# Optimizing a Trainium2 kernel written in Bass

```python
import numpy as np
import jax
import jax.numpy as jnp

def _softmax(x, axis=-1):
    return jax.nn.softmax(x, axis=axis)

def _gelu(x):
    return jax.nn.gelu(x, approximate=True)

def _silu(x):
    return jax.nn.silu(x)

def _sigmoid(x):
    return jax.nn.sigmoid(x)

def _layernorm(x, axis=-1, eps=1e-05):
    m = jnp.mean(x, axis=axis, keepdims=True)
    v = jnp.var(x, axis=axis, keepdims=True)
    return (x - m) / jnp.sqrt(v + eps)

def _scatter_add(tgt, idx, src, axis=0):
    return tgt.at[idx].add(src)

def _segment_sum(src, seg, n):
    return jax.ops.segment_sum(src, seg, n)
kernel_name = 'mk_adj_preln_d1_adj_r2_5bb64c'

def setup_inputs(seed: int=0):
    np.random.seed(seed)
    _w = jnp.asarray

    def _rec_inputs():
        import jax
        import jax.numpy as jnp
        _gk = jax.random.key(seed)
        x = 7.22e-05 + 1 * jax.random.normal(jax.random.fold_in(_gk, 1), (32, 256, 128), jnp.float32)
        _a = jax.random.bernoulli(jax.random.fold_in(_gk, 2), 0.0625, (32, 256, 256))
        _a = jnp.logical_or(_a, jnp.swapaxes(_a, -1, -2))
        _a = jnp.logical_or(_a, jnp.eye(256, dtype=bool))
        _af = _a.astype(jnp.float32)
        adj = _af
        return (x, adj)
    x, adj = _rec_inputs()

    def _L0_gnn_setup():
        import jax, jax.numpy as jnp
        import numpy as np
        from jax import lax
        DIM = 128
        EPS = 1e-05

        def _bn(h, g, b, m, v):
            scale = g / jnp.sqrt(v + EPS)
            return h * scale[None, :, None] + (b - m * scale)[None, :, None]

        def _conv1d(h, w, pad):
            return lax.conv_general_dilated(h, w, window_strides=(1,), padding=[(pad, pad)], dimension_numbers=('NCH', 'OIH', 'NCH'))
        key = jax.random.key(seed)
        ks = jax.random.split(key, 16)
        bs, n, d = (16, 1024, DIM)
        s = 0.05
        return {'x': jax.random.normal(ks[0], (bs, n, d), jnp.float32), 'mask': jnp.ones((bs, n, n), jnp.float32), 'w_se': jax.random.normal(ks[1], (3, d), jnp.float32) * s, 'b_se': jnp.zeros((3,), jnp.float32), 'conv1_w': jax.random.normal(ks[2], (d, d, 1), jnp.float32) * s, 'bn1_g': jnp.ones((d,), jnp.float32), 'bn1_b': jnp.zeros((d,), jnp.float32), 'bn1_m': jnp.zeros((d,), jnp.float32), 'bn1_v': jnp.ones((d,), jnp.float32), 'conv2_w': jax.random.normal(ks[3], (d, d, 17), jnp.float32) * s, 'bn2_g': jnp.ones((d,), jnp.float32), 'bn2_b': jnp.zeros((d,), jnp.float32), 'bn2_m': jnp.zeros((d,), jnp.float32), 'bn2_v': jnp.ones((d,), jnp.float32), 'w_msg': jax.random.normal(ks[4], (d, d), jnp.float32) * s, 'b_msg': jnp.zeros((d,), jnp.float32), 'w_ih': jax.random.normal(ks[5], (3 * d, 2 * d), jnp.float32) * s, 'b_ih': jnp.zeros((3 * d,), jnp.float32), 'w_hh': jax.random.normal(ks[6], (3 * d, d), jnp.float32) * s, 'b_hh': jnp.zeros((3 * d,), jnp.float32)}
    _L0_gnn_all = _L0_gnn_setup()
    _L0_gnn_in = {k: v for k, v in _L0_gnn_all.items() if k in ('w_se', 'b_se', 'conv1_w', 'bn1_g', 'bn1_b', 'bn1_m', 'bn1_v', 'conv2_w', 'bn2_g', 'bn2_b', 'bn2_m', 'bn2_v', 'w_msg', 'b_msg', 'w_ih', 'b_ih', 'w_hh', 'b_hh')}
    del _L0_gnn_all
    return {'x': x, 'adj': adj, 'L0_gnn_w_se': _L0_gnn_in['w_se'], 'L0_gnn_b_se': _L0_gnn_in['b_se'], 'L0_gnn_conv1_w': _L0_gnn_in['conv1_w'], 'L0_gnn_bn1_g': _L0_gnn_in['bn1_g'], 'L0_gnn_bn1_b': _L0_gnn_in['bn1_b'], 'L0_gnn_bn1_m': _L0_gnn_in['bn1_m'], 'L0_gnn_bn1_v': _L0_gnn_in['bn1_v'], 'L0_gnn_conv2_w': _L0_gnn_in['conv2_w'], 'L0_gnn_bn2_g': _L0_gnn_in['bn2_g'], 'L0_gnn_bn2_b': _L0_gnn_in['bn2_b'], 'L0_gnn_bn2_m': _L0_gnn_in['bn2_m'], 'L0_gnn_bn2_v': _L0_gnn_in['bn2_v'], 'L0_gnn_w_msg': _L0_gnn_in['w_msg'], 'L0_gnn_b_msg': _L0_gnn_in['b_msg'], 'L0_gnn_w_ih': _L0_gnn_in['w_ih'], 'L0_gnn_b_ih': _L0_gnn_in['b_ih'], 'L0_gnn_w_hh': _L0_gnn_in['w_hh'], 'L0_gnn_b_hh': _L0_gnn_in['b_hh']}

def reference(x, adj, L0_gnn_w_se, L0_gnn_b_se, L0_gnn_conv1_w, L0_gnn_bn1_g, L0_gnn_bn1_b, L0_gnn_bn1_m, L0_gnn_bn1_v, L0_gnn_conv2_w, L0_gnn_bn2_g, L0_gnn_bn2_b, L0_gnn_bn2_m, L0_gnn_bn2_v, L0_gnn_w_msg, L0_gnn_b_msg, L0_gnn_w_ih, L0_gnn_b_ih, L0_gnn_w_hh, L0_gnn_b_hh):
    import jax
    import jax.numpy as jnp

    def _L0_gnn_ref(x, mask, w_se, b_se, conv1_w, bn1_g, bn1_b, bn1_m, bn1_v, conv2_w, bn2_g, bn2_b, bn2_m, bn2_v, w_msg, b_msg, w_ih, b_ih, w_hh, b_hh):
        import jax, jax.numpy as jnp
        import numpy as np
        from jax import lax
        DIM = 128
        EPS = 1e-05

        def _bn(h, g, b, m, v):
            scale = g / jnp.sqrt(v + EPS)
            return h * scale[None, :, None] + (b - m * scale)[None, :, None]

        def _conv1d(h, w, pad):
            return lax.conv_general_dilated(h, w, window_strides=(1,), padding=[(pad, pad)], dimension_numbers=('NCH', 'OIH', 'NCH'))
        d = x.shape[-1]
        xc = jnp.transpose(x, (0, 2, 1))
        h = _bn(_conv1d(xc, conv1_w, 0), bn1_g, bn1_b, bn1_m, bn1_v)
        h = jax.nn.relu(h)
        h = _bn(_conv1d(h, conv2_w, 8), bn2_g, bn2_b, bn2_m, bn2_v)
        x_conv = jnp.transpose(jax.nn.relu(h + xc), (0, 2, 1))
        s = x @ w_se.T + b_se
        sq = jnp.sum(s * s, axis=-1)
        dist = sq[:, :, None] + sq[:, None, :] - 2.0 * jnp.einsum('bnd,bmd->bnm', s, s)
        A = jnp.exp(-dist) * mask
        msg = jax.nn.relu(x @ w_msg.T + b_msg)
        x_nmp = jnp.einsum('bnm,bmd->bnd', A, msg)
        x_in = jnp.concatenate([x_conv, x_nmp], axis=-1)
        gi = x_in @ w_ih.T + b_ih
        gh = x @ w_hh.T + b_hh
        gi_r, gi_z, gi_n = (gi[..., :d], gi[..., d:2 * d], gi[..., 2 * d:])
        gh_r, gh_z, gh_n = (gh[..., :d], gh[..., d:2 * d], gh[..., 2 * d:])
        r = jax.nn.sigmoid(gi_r + gh_r)
        z = jax.nn.sigmoid(gi_z + gh_z)
        nn_ = jnp.tanh(gi_n + r * gh_n)
        return (1.0 - z) * nn_ + z * x
    h = jnp.maximum(_layernorm(x, axis=-1), 0.0)
    x = x + _L0_gnn_ref(h, adj, L0_gnn_w_se, L0_gnn_b_se, L0_gnn_conv1_w, L0_gnn_bn1_g, L0_gnn_bn1_b, L0_gnn_bn1_m, L0_gnn_bn1_v, L0_gnn_conv2_w, L0_gnn_bn2_g, L0_gnn_bn2_b, L0_gnn_bn2_m, L0_gnn_bn2_v, L0_gnn_w_msg, L0_gnn_b_msg, L0_gnn_w_ih, L0_gnn_b_ih, L0_gnn_w_hh, L0_gnn_b_hh)
    return x

_drawn_inputs = setup_inputs


def setup_inputs(seed=0):
    import zlib

    import numpy as np

    out = dict(_drawn_inputs(seed))
    spreads = {'L0_gnn_b_se': (0.0, 0.8),
     'L0_gnn_bn1_g': (1.0, 0.6),
     'L0_gnn_bn1_b': (0.0, 0.517),
     'L0_gnn_bn1_m': (0.0, 0.484),
     'L0_gnn_bn1_v': (1.0, 0.6),
     'L0_gnn_bn2_g': (1.0, 0.6),
     'L0_gnn_bn2_b': (0.0, 0.8),
     'L0_gnn_bn2_m': (0.0, 0.748),
     'L0_gnn_bn2_v': (1.0, 0.6),
     'L0_gnn_b_msg': (0.0, 0.1),
     'L0_gnn_b_ih': (0.0, 0.302),
     'L0_gnn_b_hh': (0.0, 0.39)}
    factors = {}
    for name, (base, spread) in spreads.items():
        noise = np.random.default_rng([zlib.crc32(name.encode()), seed]).standard_normal(out[name].shape)
        drawn = base * np.exp(spread * noise) if base else spread * noise
        out[name] = jnp.asarray(drawn.astype(out[name].dtype))
    for name, factor in factors.items():
        out[name] = (out[name] * factor).astype(out[name].dtype)
    return out
```

```python
from contextlib import ExitStack

import concourse.bass as bass
from concourse import mybir

F32 = mybir.dt.float32
F32R = mybir.dt.float32r
BF16 = mybir.dt.bfloat16
ALU = mybir.AluOpType
ACT = mybir.ActivationFunctionType
AX = mybir.AxisListType

P = 128
GB = 4
EPS = 1e-5
TAPS = 17
HALO = TAPS // 2
LEAVES = 3
A, B, C = range(LEAVES)
MS = 132
SLOT = 32
ROWS = 5
KDIST = 4 * ROWS

(T0, T1, C0, C1, M0, M1, M2, SR, J0, D0, J1, D1, J2, D2, J3, D3, N0, N1) = range(18)
J = (J0, J1, J2, J3)
D = (D0, D1, D2, D3)
FRONT = 18
(CV_BB, CV_B, CV_AB, CV_A, CV_CB, CV_C) = range(6)
CONV = 6


def leaf_taps():
    even = {A: (TAPS + 1) // 2, B: (TAPS + 1) // 2, C: TAPS // 2}
    place, at = {}, 0
    for s in (A, B, C):
        for leaf in (A, B, C):
            n = even[s] // 2 if leaf == C else (even[s] + 1) // 2
            place[s, leaf] = (at, n)
            at += n
    return place, at


def build(nc, x, adj, w_se, b_se, conv1_w, bn1_g, bn1_b, bn1_m, bn1_v, conv2_w, bn2_g, bn2_b,
          bn2_m, bn2_v, w_msg, b_msg, w_ih, b_ih, w_hh, b_hh, out):
    graphs, nodes, feats = x.shape
    assert feats == P and nodes == 2 * P and graphs % (2 * GB) == 0
    groups = graphs // GB
    tiles = GB * nodes // P
    half_tiles = tiles // 2
    quarter = nodes // 4
    xw = (nodes + 2 * HALO) // 2
    lw = xw // 2
    leaf_at, n_filters = leaf_taps()
    SEC = GB * lw

    ctx = ExitStack()
    with ctx:
        def sb(name, shape, dt=F32):
            return ctx.enter_context(nc.sbuf_tensor(name, shape, dt))

        def sem(name):
            return ctx.enter_context(nc.semaphore(name))

        x_ring = sb("x_ring", [P, 4 * tiles * P])
        hn = [sb(f"hn{i}", [P, tiles, P]) for i in range(2)]
        hT = [sb(f"hT{i}", [P, tiles * P]) for i in range(2)]
        hT_hi = [sb(f"hT_hi{i}", [P, tiles * P], F32R) for i in range(2)]
        hT_lo = [sb(f"hT_lo{i}", [P, tiles * P], F32R) for i in range(2)]
        Xe = sb("Xe", [P, GB, xw])
        sect = sb("sect", [P, LEAVES, GB, xw])
        diff = sb("diff", [P, 2, LEAVES * GB, lw])
        leaf_hi = sb("leaf_hi", [P, LEAVES, LEAVES * GB, lw], F32R)
        leaf_lo = sb("leaf_lo", [P, LEAVES, LEAVES * GB, lw], F32R)
        LEAF_SLOT = {A: 0, C: 1, B: 2}
        filt_hi = sb("filt_hi", [P, n_filters, P], F32R)
        filt_lo = sb("filt_lo", [P, n_filters, P], F32R)
        c1_hi = sb("c1_hi", [P, P], F32R)
        c1_lo = sb("c1_lo", [P, P], F32R)
        w_ms = sb("w_ms", [P, MS])
        gate_hi = sb("gate_hi", [P, 3, 3 * P], F32R)
        gate_lo = sb("gate_lo", [P, 3, 3 * P], F32R)
        GX, GN, GH = range(3)
        ident = sb("ident", [P, P])
        ones_bf = sb("ones_bf", [P, P], BF16)
        BIAS_W = 4 * P + MS
        bias_parts = sb("bias_parts", [P, BIAS_W], BF16)
        scratch = sb("scratch", [P, 6400])
        xc_hi = sb("xc_hi", [P, tiles * P], F32R)
        xc_lo = sb("xc_lo", [P, tiles * P], F32R)
        nm_hi = sb("nm_hi", [P, tiles * P], F32R)
        nm_lo = sb("nm_lo", [P, tiles * P], F32R)
        adj_sb = sb("adj_sb", [P, GB, 2, nodes])
        edge = sb("edge", [P, GB, 2, nodes])
        msg = sb("msg", [P, tiles, P])
        stage = sb("stage", [P, 2, 2, GB, SLOT])
        rows = sb("rows", [P, 4 * P], F32R)
        stats = sb("stats", [P, tiles, 6])
        spread = sb("spread", [P, tiles])
        mean = sb("mean", [P, tiles])
        veps = sb("veps", [P, tiles])
        rstd = sb("rstd", [P, tiles])
        neg_half = sb("neg_half", [P, tiles])
        coord = sb("coord", [P, tiles, 3])
        coord2 = sb("coord2", [P, tiles, 3])
        dist_f = sb("dist_f", [P, 2, 2, GB, ROWS])
        bn = sb("bn", [P, 2, 4])
        bn_s = sb("bn_s", [P, 4, 2])

        off = 0

        def carve(n):
            nonlocal off
            off += n
            return scratch[:, off - n:off]
        rz = carve(tiles * 2 * P).rearrange("p (t c) -> p t c", t=tiles)
        q = carve(tiles * P).rearrange("p (t c) -> p t c", t=tiles)
        dd = carve(tiles * P).rearrange("p (t c) -> p t c", t=tiles)
        ysum = carve(tiles * P)
        pcopy = carve(3 * GB * quarter).rearrange("p (s c) -> p s c", s=3)
        m_b = carve(2 * GB * quarter)
        off = 0
        raw2 = carve(TAPS * P)
        w2T = carve(TAPS * P).rearrange("p (k o) -> p k o", k=TAPS)
        fb = carve((TAPS + 1) // 2 * P).rearrange("p (k o) -> p k o", o=P)
        fsum = raw2[:, 0:14 * P].rearrange("p (k o) -> p k o", o=P)
        edge_flat = edge[:].rearrange("p b t n -> p (b t n)")
        raw_ih = edge_flat[:, 0:6 * P].rearrange("p (g c) -> p g c", g=3)
        raw_hh = edge_flat[:, 6 * P:9 * P].rearrange("p (g c) -> p g c", g=3)
        raw_c1 = edge_flat[:, 9 * P:10 * P]
        raw_msg = edge_flat[:, 10 * P:11 * P]
        raw_se = edge_flat[0:3, 11 * P:12 * P]
        row0 = msg[0:1, :, :].rearrange("p t c -> p (t c)")
        bias_row = row0[:, 0:BIAS_W]
        bhh_row = sb("bhh_row", [1, 3 * P])
        part_row = sb("part_row", [1, BIAS_W], BF16)

        cb = [ctx.enter_context(nc.psum_tensor(f"conv_bank{i}", [P, 512], F32)) for i in range(3)]
        gbk = [ctx.enter_context(nc.psum_tensor(f"gate_bank{i}", [P, 512], F32)) for i in range(2)]
        fbk = [ctx.enter_context(nc.psum_tensor(f"front_bank{i}", [P, 512], F32)) for i in range(3)]

        x_in = [sem(f"x_in{i}") for i in range(2)]
        adj_in = [sem(f"adj_in{b}") for b in range(GB)]
        out_stored = [sem(f"out_stored{h}") for h in range(2)]
        w_in = sem("w_in")
        w2_in = sem("w2_in")
        front_done = sem("front_done")
        conv_done = sem("conv_done")
        gate_done = sem("gate_done")
        w_turned = sem("w_turned")
        hT_ready = sem("hT_ready")
        h1_ready = sem("h1_ready")
        p_copied = sem("p_copied")
        msg_ready = sem("msg_ready")
        rows_ready = sem("rows_ready")
        exp_ready = sem("exp_ready")
        xc_hi_ready = sem("xc_hi_ready")
        leaf_hi_ready = sem("leaf_hi_ready")
        rz_ready = sem("rz_ready")
        n_ready = sem("n_ready")
        nm_hi_ready = sem("nm_hi_ready")
        ln_link = sem("ln_link")
        veps_ready = sem("veps_ready")
        hn_ready = sem("hn_ready")
        hT_split = sem("hT_split")
        mb_ready = sem("mb_ready")
        y_ready = sem("y_ready")
        coord_ready = sem("coord_ready")
        row_link = sem("row_link")
        stage_ready = sem("stage_ready")
        edge_ready = sem("edge_ready")
        xc_lo_ready = sem("xc_lo_ready")
        leaf_lo_ready = sem("leaf_lo_ready")
        m_ready = sem("m_ready")
        q_ready = sem("q_ready")
        d_ready = sem("d_ready")
        out_ready = sem("out_ready")
        nm_lo_ready = sem("nm_lo_ready")
        rstd_ready = sem("rstd_ready")
        q_res = sem("q_res")
        diff_ready = sem("diff_ready")
        p_ready = sem("p_ready")
        ident_ready = sem("ident_ready")
        pool_link = sem("pool_link")
        zero_ready = sem("zero_ready")
        bn_veps = sem("bn_veps")
        bn_powed = sem("bn_powed")
        bn_ready = sem("bn_ready")
        raw_scaled = sem("raw_scaled")
        small_hi = sem("small_hi")
        small_ready = sem("small_ready")
        taps_a = sem("taps_a")
        taps_v = sem("taps_v")
        sums_ready = sem("sums_ready")
        filt_hi_ready = sem("filt_hi_ready")
        filt_lo_ready = sem("filt_lo_ready")
        bias_link = sem("bias_link")

        block = ctx.enter_context(nc.Block())

        def wait(eng, s, value):
            if not isinstance(value, int) or value > 0:
                eng.wait_ge(s, value)

        def steps(eng, step):
            step(0, 0, True, False)
            step(0, 1, True, True)
            with eng.Fori(1, groups // 2) as it:
                for par in range(2):
                    step(it, par, True, True)
            step(groups // 2, 0, False, True)

        def slot(it, par):
            return ((it % 2) * 2 + par) * (tiles * P)

        def slot_before(it, par):
            return slot(it, 0) if par else (((it + 1) % 2) * 2 + 1) * (tiles * P)

        ZEROS, TURNED, LINKS, BIAS_LINKS, NORM_LINKS = 9, 8, 7, 12, 7
        SMALL_LOADS = 18
        SUM_AT = {A: 0, B: 5, C: 10}

        def phases(ap, l1):
            return ap.rearrange("p (b i l m) -> p l b i m", b=GB, i=quarter, l=2)[:, :, :, :, l1]

        def by_phase(ap):
            return ap.rearrange("p (l b i) -> p l b i", l=2, b=GB)

        def for_both(ap):
            return ap.rearrange("p (l b i) -> p l b i", l=1, b=GB).broadcast_to([P, 2, GB, quarter])

        def half_of(ap, h):
            return ap[:, h * half_tiles:(h + 1) * half_tiles, :].rearrange("p t c -> p (t c)")

        def ms_bank(n, nt):
            return fbk[(M0 + n) % 3][:, 0:nt * MS].rearrange("p (t c) -> p t c", c=MS)

        samples = sect[:].rearrange("p s b n -> p (s b) n")

        def half_run(s, first, n):
            if s == B:
                return fb[:, first:first + 2 * n - 1:2, :]
            k = 2 * first + (s == C)
            return w2T[:, k:k + 4 * n - 3:4, :]

        def leaf_source(s, leaf):
            n = leaf_at[s, leaf][1]
            if leaf == A:
                return half_run(s, 0, n)
            if leaf == C:
                return half_run(s, 1, n)
            return fsum[:, SUM_AT[s]:SUM_AT[s] + n, :]

        @block.sync
        def _(sp):
            def load_x(it, par, g):
                at = slot(it, par)
                sp.dma_start(x_ring[:, bass.ds(at, tiles * P)].rearrange("p (b t c) -> p b t c", b=GB, t=2),
                             x_groups[g]).then_inc(x_in[par], 16)

            x_groups = x.rearrange("(g b) (t p) c -> g p b t c", b=GB, p=P)
            o_groups = out.rearrange("(g b) (t p) c -> g p b t c", b=GB, p=P)
            a_graphs = adj.rearrange("(g b) (t p) m -> g b p t m", b=GB, p=P)

            def step(it, par, front, back, load):
                g = 2 * it + par
                at = slot_before(it, par)
                if front:
                    for b in range(GB):
                        wait(sp, front_done, FRONT * (g - 1) + J[b] + 1)
                        sp.dma_start(adj_sb[:, b, :, :], a_graphs[g, b]).then_inc(adj_in[b], 16)
                if back:
                    for h in range(2):
                        wait(sp, out_stored[h], 16 * (g - 1))
                if load:
                    sp.wait_ge(hn_ready, 2 * g + 2)
                    load_x(it + 1, par, g + 2)
                if back:
                    for h in range(2):
                        sp.wait_ge(out_ready, 2 * (g - 1) + h + 1)
                        half = GB // 2
                        sp.dma_start(
                            o_groups[g - 1][:, half * h:half * h + half],
                            x_ring[:, bass.ds(at + h * half_tiles * P, half_tiles * P)]
                            .rearrange("p (b t c) -> p b t c", b=half, t=2),
                        ).then_inc(out_stored[h], 16)

            load_x(0, 0, 0)
            load_x(0, 1, 1)
            step(0, 0, True, False, True)
            step(0, 1, True, True, True)
            with sp.Fori(1, groups // 2 - 1) as it:
                for par in range(2):
                    step(it, par, True, True, True)
            step(groups // 2 - 1, 0, True, True, False)
            step(groups // 2 - 1, 1, True, True, False)
            step(groups // 2, 0, False, True, False)
            for h in range(2):
                sp.wait_ge(out_stored[h], 16 * groups)

        @block.gpsimd
        def _(pool):
            pool.memset(ident[:], 0.0).then_inc(pool_link, 1)
            pool.wait_ge(pool_link, 1)
            pool.affine_select(out=ident[:], in_=ident[:], compare_op=ALU.not_equal, fill=1.0, base=0,
                               pattern=[[-1, P]], channel_multiplier=1).then_inc(ident_ready, 1)
            pool.memset(neg_half[:], -0.5).then_inc(zero_ready, 1)
            pool.memset(Xe[:], 0.0).then_inc(zero_ready, 1)
            pool.memset(sect[:], 0.0).then_inc(zero_ready, 1)
            pool.memset(diff[:], 0.0).then_inc(zero_ready, 1)
            pool.memset(stage[:], 0.0).then_inc(zero_ready, 1)
            pool.memset(ones_bf[:], 1.0).then_inc(zero_ready, 1)
            pool.memset(bias_parts[:], 0.0).then_inc(zero_ready, 1)
            pool.memset(dist_f[:, 0, :, :, 3:4], -1.0).then_inc(zero_ready, 1)
            pool.memset(dist_f[:, 1, :, :, 4:5], 1.0).then_inc(zero_ready, 1)
            pool.wait_ge(zero_ready, ZEROS)
            pool.wait_ge(bn_veps, 1)
            pool.tensor_tensor(bn_s[:, 1], bn_s[:, 0], neg_half[:, 0:2], ALU.pow).then_inc(bn_powed, 1)

            def step(it, par, front, back):
                g = 2 * it + par
                gb = g - 1
                if front:
                    pool.wait_ge(veps_ready, g + 1)
                    wait(pool, hn_ready, 2 * g)
                    pool.tensor_tensor(rstd[:], veps[:], neg_half[:], ALU.pow).then_inc(rstd_ready, 1)
                if back:
                    pool.wait_ge(mb_ready, gb + 1)
                    wait(pool, xc_hi_ready, gb)
                    wait(pool, xc_lo_ready, gb)
                    for l1 in range(2):
                        pool.tensor_tensor(phases(ysum, l1), phases(hT[1 - par][:], l1), by_phase(m_b),
                                           ALU.add).then_inc(q_res, 1)
                    pool.wait_ge(p_copied, 3 * gb + 2)
                    pool.wait_ge(q_res, 4 * gb + 1)
                    pool.tensor_tensor(phases(ysum, 0), phases(ysum, 0), for_both(pcopy[:, 1, :]),
                                       ALU.add).then_inc(q_res, 1)
                if front:
                    pool.wait_ge(h1_ready, 4 * g + 4)
                    pool.tensor_tensor(sect[:, A], Xe[:], sect[:, B], ALU.subtract).then_inc(diff_ready, 1)
                    pool.tensor_tensor(sect[:, C, :, 0:xw - 1], Xe[:, :, 1:xw], sect[:, B, :, 0:xw - 1],
                                       ALU.subtract).then_inc(diff_ready, 1)
                if back:
                    pool.wait_ge(p_copied, 3 * gb + 3)
                    pool.wait_ge(q_res, 4 * gb + 2)
                    pool.tensor_tensor(phases(ysum, 1), phases(ysum, 1), for_both(pcopy[:, 2, :]),
                                       ALU.add).then_inc(q_res, 1)
                if front:
                    pool.wait_ge(diff_ready, 4 * g + 2)
                    wait(pool, leaf_hi_ready, 2 * g)
                    wait(pool, leaf_lo_ready, 2 * g)
                    pool.tensor_tensor(diff[:, 0], samples[:, :, 0:xw:2], samples[:, :, 1:xw:2],
                                       ALU.subtract).then_inc(diff_ready, 1)
                    pool.tensor_tensor(diff[:, 1, :, 0:lw - 1], samples[:, :, 2:xw:2],
                                       samples[:, :, 1:xw - 2:2], ALU.subtract).then_inc(diff_ready, 1)
                if back:
                    at = slot_before(it, par)
                    for h in range(2):
                        pool.wait_ge(n_ready, 2 * gb + h + 1)
                        part = x_ring[:, bass.ds(at + h * half_tiles * P, half_tiles * P)]
                        pool.tensor_tensor(part, part, half_of(q, h), ALU.add).then_inc(p_ready, 1)

            steps(pool, step)

        @block.scalar
        def _(act):
            def row(vec):
                return vec.rearrange("(a n) -> a n", a=1)

            def column(vec):
                return vec.rearrange("(p a) -> p a", a=1)

            loads = [(raw_c1, conv1_w.rearrange("o i k -> o (i k)")), (raw_msg, w_msg)]
            loads += [(bn[:, n, k:k + 1], column(vec)) for n, vecs in enumerate(
                ((bn1_g, bn1_b, bn1_m, bn1_v), (bn2_g, bn2_b, bn2_m, bn2_v))) for k, vec in enumerate(vecs)]
            loads += [(raw_hh, w_hh.rearrange("(g o) c -> o g c", g=3)),
                      (raw_ih, w_ih.rearrange("(g o) c -> o g c", g=3)),
                      (raw_se, w_se),
                      (bias_row[:, 0:P], row(b_ih[2 * P:3 * P])), (bias_row[:, P:3 * P], row(b_ih[0:2 * P])),
                      (bias_row[:, 4 * P:5 * P], row(b_msg)), (bias_row[:, 5 * P:5 * P + 3], row(b_se)),
                      (bhh_row[:], row(b_hh))]
            assert len(loads) == SMALL_LOADS
            for dst, src in loads:
                act.dma_start(dst, src).then_inc(w_in, 16)
            act.dma_start(raw2, conv2_w.rearrange("o i k -> o (i k)")).then_inc(w2_in, 16)

            for n, (dst, bank, width) in enumerate(((c1_hi[:], fbk[0], P), (gate_hi[:, GX], fbk[1], 3 * P),
                                                    (gate_hi[:, GN], fbk[2], 3 * P),
                                                    (gate_hi[:, GH], gbk[0], 3 * P))):
                act.wait_ge(w_turned, n + 1)
                act.activation(dst, bank[:, 0:width], ACT.Copy).then_inc(small_hi, 1)
            for n in (1, 2):
                act.wait_ge(w_turned, TURNED - 2 + n)
                act.activation(w2T[:, 4 * n + 4:4 * n + 8, :].rearrange("p k o -> p (k o)"), cb[n][:],
                               ACT.Copy).then_inc(taps_a, 1)

            def edges(g, b):
                act.wait_ge(front_done, FRONT * g + D[b] + 1)
                act.activation(edge[:, b].rearrange("p t n -> p (t n)"), fbk[D[b] % 3][:],
                               ACT.Exp).then_inc(exp_ready, 1)

            def shared(gb, n, kind):
                act.wait_ge(conv_done, CONV * gb + kind + 1)
                if n == 0:
                    wait(act, mb_ready, gb)
                    act.activation(pcopy[:, 0, :], cb[kind % 3][:, 0:GB * quarter], ACT.Identity,
                                   bias=bn_s[:, 3, 1:2]).then_inc(p_copied, 1)
                else:
                    wait(act, q_res, 4 * gb)
                    act.activation(pcopy[:, n, :], cb[kind % 3][:, 0:GB * quarter],
                                   ACT.Copy).then_inc(p_copied, 1)

            def step(it, par, front, back):
                g = 2 * it + par
                gb = g - 1
                first = isinstance(it, int) and it == 0 and par == 0
                if back:
                    shared(gb, 0, CV_BB)
                    shared(gb, 1, CV_AB)
                if front:
                    wait(act, front_done, FRONT * (g - 2) + M2 + 1)
                    wait(act, hT_split, 4 * (g - 1))
                    wait(act, q_res, 4 * (g - 1))
                    for h in range(2):
                        act.wait_ge(front_done, FRONT * g + T0 + h + 1)
                        act.activation(hT[par][:, h * 512:(h + 1) * 512], fbk[(T0 + h) % 3][:],
                                       ACT.Relu).then_inc(hT_ready, 1)
                    wait(act, diff_ready, 4 * g)
                    wait(act, leaf_lo_ready, 2 * g)
                    wait(act, leaf_hi_ready, 2 * g)
                    if first:
                        act.wait_ge(bn_ready, 4)
                        act.wait_ge(zero_ready, ZEROS)
                    for h in range(2):
                        act.wait_ge(front_done, FRONT * g + C0 + h + 1)
                        v = fbk[(C0 + h) % 3][:].rearrange("p (b n m) -> p b n m", b=2, m=2)
                        pad = HALO // 2
                        for m, dst in ((0, Xe[:, 2 * h:2 * h + 2]), (1, sect[:, B, 2 * h:2 * h + 2])):
                            act.activation(dst[:, :, pad:pad + nodes // 2], v[:, :, :, m], ACT.Relu,
                                           bias=bn_s[:, 3, 0:1]).then_inc(h1_ready, 1)
                if back:
                    shared(gb, 2, CV_CB)
                if front:
                    wait(act, front_done, FRONT * g)
                    if first:
                        act.wait_ge(bias_link, BIAS_LINKS)
                    for n in range(3):
                        act.wait_ge(front_done, FRONT * g + M0 + n + 1)
                        nt = min(3, tiles - 3 * n)
                        act.activation(msg[:, 3 * n:3 * n + nt, :], ms_bank(n, nt)[:, :, 0:P],
                                       ACT.Relu).then_inc(msg_ready, 1)
                    act.wait_ge(front_done, FRONT * g + SR + 1)
                    act.activation(rows[:], fbk[SR % 3][:], ACT.Copy).then_inc(rows_ready, 1)
                    edges(g, 0)
                if back:
                    wait(act, gate_done, tiles * gb)
                    act.wait_ge(y_ready, 2 * gb + 2)
                    act.activation(xc_hi[:], ysum, ACT.Relu).then_inc(xc_hi_ready, 1)
                if front:
                    edges(g, 1)
                    wait(act, conv_done, CONV * g)
                    act.wait_ge(diff_ready, 4 * g + 4)
                    act.activation(leaf_hi[:, 0:2], diff[:], ACT.Copy).then_inc(leaf_hi_ready, 1)
                    act.activation(leaf_hi[:, 2], samples[:, :, 1:xw:2], ACT.Copy).then_inc(leaf_hi_ready, 1)
                for t in range(tiles):
                    if back:
                        act.wait_ge(gate_done, tiles * gb + t + 1)
                        if t == 0:
                            wait(act, d_ready, 4 * gb)
                        act.activation(rz[:, t, :], gbk[t % 2][:, P:3 * P], ACT.Tanh,
                                       scale=0.5).then_inc(rz_ready, 1)
                    if front and t in (3, 5):
                        edges(g, 2 if t == 3 else 3)
                    if back and t == 5:
                        new_state(gb, 0)
                if back:
                    new_state(gb, 1)
                if front:
                    wait(act, gate_done, tiles * g)
                    for h in range(2):
                        act.wait_ge(front_done, FRONT * g + N0 + h + 1)
                        act.activation(nm_hi[:, h * 512:(h + 1) * 512], fbk[(N0 + h) % 3][:],
                                       ACT.Copy).then_inc(nm_hi_ready, 1)
                if first:
                    act.wait_ge(sums_ready, 3)
                    for n, key in enumerate(sorted(leaf_at)):
                        at, k = leaf_at[key]
                        act.activation(filt_hi[:, at:at + k, :], leaf_source(*key), ACT.Copy)\
                           .then_inc(filt_hi_ready, 1)

            def new_state(gb, h):
                act.wait_ge(q_ready, tiles * gb + half_tiles * (h + 1))
                act.activation(half_of(q, h), half_of(q, h), ACT.Tanh).then_inc(n_ready, 1)

            steps(act, step)

        @block.vector
        def _(dve):
            dve.wait_ge(w_in, 16 * SMALL_LOADS)
            dve.tensor_scalar(bn_s[:, 0], bn[:, :, 3], EPS, None, ALU.add).then_inc(bn_veps, 1)
            dve.wait_ge(bn_powed, 1)
            dve.tensor_tensor(bn_s[:, 2], bn[:, :, 0], bn_s[:, 1], ALU.mult).then_inc(bn_ready, 1)
            dve.wait_ge(bn_ready, 1)
            dve.tensor_tensor(bn_s[:, 3], bn[:, :, 2], bn_s[:, 2], ALU.mult).then_inc(bn_ready, 1)
            dve.wait_ge(bn_ready, 2)
            dve.tensor_tensor(bn_s[:, 3], bn[:, :, 1], bn_s[:, 3], ALU.subtract).then_inc(bn_ready, 1)
            dve.tensor_scalar(raw_hh[:, 2, :], raw_hh[:, 2, :], 0.5, None, ALU.mult).then_inc(bn_ready, 1)
            dve.tensor_scalar(raw_c1, raw_c1, bn_s[:, 2, 0:1], None, ALU.mult).then_inc(raw_scaled, 1)
            dve.wait_ge(w2_in, 16)
            dve.tensor_scalar(raw2, raw2, bn_s[:, 2, 1:2], None, ALU.mult).then_inc(raw_scaled, 1)

            def lo_part(out_ap, src, hi):
                return dve.tensor_tensor(out_ap, src, hi.bitcast(F32), ALU.subtract)

            dve.memset(bias_row[:, BIAS_W - 1:BIAS_W], 0.0).then_inc(bias_link, 1)
            dve.tensor_tensor(bias_row[:, P:3 * P], bias_row[:, P:3 * P], bhh_row[:, 0:2 * P],
                              ALU.add).then_inc(bias_link, 1)
            dve.tensor_scalar(bias_row[:, 3 * P:4 * P], bhh_row[:, 2 * P:3 * P], 0.5, None,
                              ALU.mult).then_inc(bias_link, 1)
            dve.wait_ge(zero_ready, ZEROS)
            n = 3
            for k in range(3):
                dve.wait_ge(bias_link, n)
                dve.tensor_copy(part_row[:], bias_row).then_inc(bias_link, 1)
                dve.wait_ge(bias_link, n + 1)
                dve.tensor_copy(bias_parts[32 * k:32 * k + 1, :], part_row[:]).then_inc(bias_link, 1)
                dve.tensor_tensor(bias_row, bias_row, part_row[:], ALU.subtract).then_inc(bias_link, 1)
                n += 3

            for n, (dst, bank, hi) in enumerate(((c1_lo[:], fbk[0], c1_hi[:]),
                                                 (gate_lo[:, GX], fbk[1], gate_hi[:, GX]),
                                                 (gate_lo[:, GN], fbk[2], gate_hi[:, GN]),
                                                 (gate_lo[:, GH], gbk[0], gate_hi[:, GH]))):
                dve.wait_ge(small_hi, n + 1)
                lo_part(dst, bank[:, 0:hi.shape[-1]], hi).then_inc(small_ready, 1)
                if n == 0:
                    dve.memset(w_ms[:, MS - 1:MS], 0.0).then_inc(small_ready, 1)
                    dve.tensor_copy(w_ms[:, 0:MS - 1], fbk[0][:, P:P + MS - 1]).then_inc(small_ready, 1)
            dve.tensor_copy(w2T[:, TAPS - 1, :], gbk[0][:, 3 * P:4 * P]).then_inc(taps_v, 1)
            for n, bank in enumerate((gbk[1], cb[0])):
                dve.wait_ge(w_turned, TURNED - 3 + n)
                dve.tensor_copy(w2T[:, 4 * n:4 * n + 4, :].rearrange("p k o -> p (k o)"),
                                bank[:]).then_inc(taps_v, 1)

            def filters():
                dve.wait_ge(taps_a, 2)
                dve.wait_ge(taps_v, 3)
                dve.tensor_tensor(fb[:, 0:TAPS // 2, :], w2T[:, 0:TAPS - 1:2, :], w2T[:, 1:TAPS:2, :],
                                  ALU.add).then_inc(taps_v, 1)
                dve.tensor_copy(fb[:, TAPS // 2, :], w2T[:, TAPS - 1, :]).then_inc(taps_v, 1)
                dve.wait_ge(taps_v, 5)
                for s in (A, B, C):
                    n_even, n_odd = leaf_at[s, A][1], leaf_at[s, C][1]
                    if n_even > n_odd:
                        dve.tensor_copy(fsum[:, SUM_AT[s] + n_odd, :], half_run(s, 0, n_even)[:, n_odd, :])
                    dve.tensor_tensor(fsum[:, SUM_AT[s]:SUM_AT[s] + n_odd, :], half_run(s, 0, n_odd),
                                      half_run(s, 1, n_odd), ALU.add).then_inc(sums_ready, 1)
                for n, key in enumerate(sorted(leaf_at)):
                    at, k = leaf_at[key]
                    dve.wait_ge(filt_hi_ready, n + 1)
                    lo_part(filt_lo[:, at:at + k, :], leaf_source(*key),
                            filt_hi[:, at:at + k, :]).then_inc(filt_lo_ready, 1)

            def norm_stats(it, par, g):
                dve.wait_ge(x_in[par], 16 * (it + 1))
                at = slot(it, par)
                for t in range(tiles):
                    last = dve.bn_stats(stats[:, t, :], x_ring[:, bass.ds(at + t * P, P)])
                last.then_inc(ln_link, 1)
                mean_e, m2_e, mean_o, m2_o = (stats[:, :, k] for k in (1, 2, 4, 5))
                dve.wait_ge(ln_link, NORM_LINKS * g + 1)
                dve.tensor_tensor(spread[:], mean_e, mean_o, ALU.subtract).then_inc(ln_link, 1)
                dve.tensor_tensor(mean[:], mean_e, mean_o, ALU.add).then_inc(ln_link, 1)
                dve.tensor_tensor(veps[:], m2_e, m2_o, ALU.add).then_inc(ln_link, 1)
                dve.wait_ge(ln_link, NORM_LINKS * g + 4)
                dve.tensor_tensor(spread[:], spread[:], spread[:], ALU.mult).then_inc(ln_link, 1)
                dve.tensor_scalar(mean[:], mean[:], 0.5, None, ALU.mult).then_inc(ln_link, 1)
                dve.tensor_scalar(veps[:], veps[:], 1.0 / P, EPS, ALU.mult, ALU.add).then_inc(ln_link, 1)
                dve.wait_ge(ln_link, NORM_LINKS * g + 7)
                dve.scalar_tensor_tensor(veps[:], spread[:], 0.25, veps[:], ALU.mult,
                                         ALU.add).then_inc(veps_ready, 1)

            def normalise(it, par, g):
                dve.wait_ge(rstd_ready, g + 1)
                wait(dve, front_done, FRONT * (g - 2) + T1 + 1)
                at = slot(it, par)
                for t in range(tiles):
                    last = dve.tensor_scalar(hn[par][:, t, :], x_ring[:, bass.ds(at + t * P, P)],
                                             mean[:, t:t + 1], rstd[:, t:t + 1], ALU.subtract, ALU.mult)
                    if t % half_tiles == half_tiles - 1:
                        last.then_inc(hn_ready, 1)

            def split_nodes(par, g):
                wait(dve, gate_done, tiles * (g - 1))
                for h in range(2):
                    cols = slice(h * 512, (h + 1) * 512)
                    dve.wait_ge(hT_ready, 2 * g + h + 1)
                    dve.tensor_copy(hT_hi[par][:, cols], hT[par][:, cols]).then_inc(hT_split, 1)
                    dve.wait_ge(hT_split, 4 * g + 2 * h + 1)
                    lo_part(hT_lo[par][:, cols], hT[par][:, cols], hT_hi[par][:, cols])\
                        .then_inc(hT_split, 1)

            def section_b(gb):
                dve.wait_ge(conv_done, CONV * gb + CV_B + 1)
                dve.wait_ge(p_copied, 3 * gb + 1)
                wait(dve, q_res, 4 * gb)
                dve.tensor_tensor(m_b.rearrange("p (l c) -> p l c", l=2),
                                  cb[CV_B % 3][:].rearrange("p (l c) -> p l c", l=2),
                                  pcopy[:, 0:1, :].broadcast_to([P, 2, GB * quarter]),
                                  ALU.add).then_inc(mb_ready, 1)

            def outputs(gb, l1):
                kind = (CV_A, CV_C)[l1]
                dve.wait_ge(conv_done, CONV * gb + kind + 1)
                dve.wait_ge(q_res, 4 * gb + 3 + l1)
                dve.tensor_tensor(phases(ysum, l1), by_phase(cb[kind % 3][:]), phases(ysum, l1),
                                  ALU.add).then_inc(y_ready, 1)

            def distance_rows(g):
                for n in range(3):
                    nt = min(3, tiles - 3 * n)
                    dve.wait_ge(msg_ready, 3 * g + n + 1)
                    dve.tensor_copy(coord[:, 3 * n:3 * n + nt, :],
                                    ms_bank(n, nt)[:, :, P:P + 3]).then_inc(coord_ready, 1)
                dve.wait_ge(coord_ready, 3 * g + 3)
                turned = coord[:].rearrange("p (b t) c -> p t b c", t=2)
                links = LINKS * g
                dve.tensor_tensor(coord2[:], coord[:], coord[:], ALU.mult).then_inc(row_link, 1)
                dve.tensor_scalar(dist_f[:, 0, :, :, 0:3], turned, 2.0, None, ALU.mult).then_inc(row_link, 1)
                dve.tensor_copy(dist_f[:, 1, :, :, 0:3], turned).then_inc(row_link, 1)
                dve.wait_ge(row_link, links + 3)
                dve.reduce_sum(dist_f[:, 1, :, :, 3], coord2[:].rearrange("p (b t) c -> p t b c", t=2),
                               axis=AX.X).then_inc(row_link, 1)
                dve.wait_ge(row_link, links + 4)
                dve.tensor_scalar(dist_f[:, 0, :, :, 4], dist_f[:, 1, :, :, 3], -1.0, None,
                                  ALU.mult).then_inc(row_link, 1)
                dve.wait_ge(row_link, links + 5)
                wait(dve, front_done, FRONT * (g - 1) + SR + 1)
                f = dist_f[:].rearrange("p s t b r -> p (s t b) r")
                st = stage[:].rearrange("p s t b r -> p (s t b) r")
                dve.tensor_copy(st[:, :, 0:ROWS].bitcast(F32R), f).then_inc(row_link, 1)
                dve.wait_ge(row_link, links + 6)
                dve.tensor_tensor(st[:, :, 3 * ROWS:4 * ROWS], f, st[:, :, 0:ROWS],
                                  ALU.subtract).then_inc(row_link, 1)
                dve.wait_ge(row_link, links + 7)
                half = 2 * GB
                for side, dst, src in ((0, 1, 0), (0, 2, 3), (1, 2, 0), (1, 1, 3)):
                    v = st[:, side * half:(side + 1) * half, :]
                    last = dve.tensor_copy(v[:, :, dst * ROWS:(dst + 1) * ROWS],
                                           v[:, :, src * ROWS:(src + 1) * ROWS])
                last.then_inc(stage_ready, 1)

            def edge_weights(g, b):
                dve.wait_ge(exp_ready, GB * g + b + 1)
                dve.wait_ge(front_done, FRONT * g + J[b] + 1)
                v = edge[:, b].rearrange("p t n -> p (t n)")
                dve.tensor_tensor(v, fbk[J[b] % 3][:], v, ALU.mult).then_inc(edge_ready, 1)

            def split_leaves(g):
                wait(dve, conv_done, CONV * g)
                dve.wait_ge(leaf_hi_ready, 2 * g + 1)
                lo_part(leaf_lo[:, 0:2], diff[:], leaf_hi[:, 0:2]).then_inc(leaf_lo_ready, 1)
                dve.wait_ge(leaf_hi_ready, 2 * g + 2)
                lo_part(leaf_lo[:, 2], samples[:, :, 1:xw:2], leaf_hi[:, 2]).then_inc(leaf_lo_ready, 1)

            def gates(gb, t):
                n = tiles * gb + t + 1
                dve.wait_ge(rz_ready, n)
                if t == 0:
                    wait(dve, p_ready, 2 * gb)
                dve.scalar_tensor_tensor(q[:, t, :], rz[:, t, 0:P], 1.0, gbk[t % 2][:, 3 * P:4 * P],
                                         ALU.add, ALU.mult).then_inc(m_ready, 1)
                dve.wait_ge(m_ready, n)
                dve.tensor_tensor(q[:, t, :], q[:, t, :], gbk[t % 2][:, 0:P], ALU.add).then_inc(q_ready, 1)

            def finish(it, par, gb, h):
                ts = slice(h * half_tiles, (h + 1) * half_tiles)
                dve.wait_ge(n_ready, 2 * gb + h + 1)
                dve.scalar_tensor_tensor(dd[:, ts, :], hn[1 - par][:, ts, :], 0.0, q[:, ts, :],
                                         ALU.max, ALU.subtract).then_inc(d_ready, 1)
                dve.wait_ge(d_ready, 4 * gb + 2 * h + 1)
                dve.scalar_tensor_tensor(dd[:, ts, :], rz[:, ts, P:2 * P], 1.0, dd[:, ts, :],
                                         ALU.add, ALU.mult).then_inc(d_ready, 1)
                dve.wait_ge(d_ready, 4 * gb + 2 * h + 2)
                dve.wait_ge(p_ready, 2 * gb + h + 1)
                part = x_ring[:, bass.ds(slot_before(it, par) + h * half_tiles * P, half_tiles * P)]
                dve.scalar_tensor_tensor(part, half_of(dd, h), 0.5, part, ALU.mult,
                                         ALU.add).then_inc(out_ready, 1)

            def step(it, par, front, back):
                g = 2 * it + par
                gb = g - 1
                if front:
                    norm_stats(it, par, g)
                if back:
                    section_b(gb)
                if front:
                    normalise(it, par, g)
                    split_nodes(par, g)
                if back:
                    outputs(gb, 0)
                if front:
                    distance_rows(g)
                if back:
                    outputs(gb, 1)
                if front:
                    edge_weights(g, 0)
                if back:
                    wait(dve, gate_done, tiles * gb)
                    dve.wait_ge(xc_hi_ready, gb + 1)
                    dve.scalar_tensor_tensor(xc_lo[:], ysum, 0.0, xc_hi[:].bitcast(F32), ALU.max,
                                             ALU.subtract).then_inc(xc_lo_ready, 1)
                if front:
                    edge_weights(g, 1)
                    split_leaves(g)
                for t in range(tiles):
                    if back:
                        gates(gb, t)
                    if front and t in (3, 5):
                        edge_weights(g, 2 if t == 3 else 3)
                    if back and t == 6:
                        finish(it, par, gb, 0)
                if back:
                    finish(it, par, gb, 1)
                if front:
                    for h in range(2):
                        cols = slice(h * 512, (h + 1) * 512)
                        dve.wait_ge(nm_hi_ready, 2 * g + h + 1)
                        lo_part(nm_lo[:, cols], fbk[(N0 + h) % 3][:], nm_hi[:, cols])\
                            .then_inc(nm_lo_ready, 1)
                if isinstance(it, int) and it == 0 and par == 0:
                    filters()

            steps(dve, step)

        @block.tensor
        def _(pe):
            def products(out_ap, pairs, start, stop):
                terms = [t for lh, ll, rh, rl in pairs for t in ((lh, rh), (lh, rl), (ll, rh))]
                for n, (lhs, rhs) in enumerate(terms):
                    last = pe.matmul(out_ap, lhs, rhs, start=start and n == 0,
                                     stop=stop and n == len(terms) - 1)
                return last

            pe.wait_ge(ident_ready, 1)
            pe.wait_ge(raw_scaled, 1)
            pe.wait_ge(bn_ready, 4)
            w_tap = raw2.rearrange("p (i k) -> p k i", k=TAPS)
            gate_order = (2, 0, 1)

            def turn(bank, sources):
                for n, src in enumerate(sources):
                    k = src.shape[0]
                    last = pe.transpose(bank[:, n * P:n * P + k], src, ident[0:k, 0:k])
                last.then_inc(w_turned, 1)

            turn(fbk[0], [raw_c1, raw_msg, raw_se])
            turn(fbk[1], [raw_ih[:, n, 0:P] for n in gate_order])
            turn(fbk[2], [raw_ih[:, n, P:2 * P] for n in gate_order])
            pe.wait_ge(raw_scaled, 2)
            turn(gbk[0], [raw_hh[:, n, :] for n in range(3)] + [w_tap[:, TAPS - 1, :]])
            for n, bank in enumerate((gbk[1], cb[0], cb[1], cb[2])):
                turn(bank, [w_tap[:, 4 * n + k, :] for k in range(4)])

            def conv(par, gb, kind, section, leaves, release, released):
                wait(pe, release, released)
                for n, leaf in enumerate(leaves):
                    at, taps = leaf_at[section, leaf]
                    pairs = []
                    for k in range(taps):
                        hi, lo = (v[:, LEAF_SLOT[leaf], section * GB:(section + 1) * GB, k:k + quarter]
                                  for v in (leaf_hi, leaf_lo))
                        pairs.append((filt_hi[:, at + k, :], filt_lo[:, at + k, :], hi, lo))
                    width = GB * quarter
                    last = products(cb[kind % 3][:, n * width:(n + 1) * width], pairs, True, True)
                last.then_inc(conv_done, 1)

            def turn_nodes(par, g):
                for h, (s, n) in enumerate(((exp_ready, GB * g), (nm_lo_ready, 2 * g - 1))):
                    wait(pe, s, n)
                    pe.wait_ge(hn_ready, 2 * g + h + 1)
                    for t in range(half_tiles):
                        last = pe.transpose(fbk[(T0 + h) % 3][:, t * P:(t + 1) * P],
                                            hn[par][:, h * half_tiles + t, :], ident[:])
                    last.then_inc(front_done, 1)

            def conv1(par, g):
                for h, (s, n) in enumerate(((nm_lo_ready, 2 * g), (hT_ready, 2 * g + 1))):
                    wait(pe, s, n)
                    pe.wait_ge(hT_split, 4 * g + 2 * h + 2)
                    cols = slice(h * 512, (h + 1) * 512)
                    products(fbk[(C0 + h) % 3][:], [(c1_hi[:], c1_lo[:], hT_hi[par][:, cols],
                                                     hT_lo[par][:, cols])], True, True)\
                        .then_inc(front_done, 1)

            def messages(par, g):
                for n, (s, v) in enumerate(((hT_ready, 2 * g + 2), (h1_ready, 4 * g + 2),
                                            (h1_ready, 4 * g + 4))):
                    pe.wait_ge(s, v)
                    for t in range(3 * n, min(3 * n + 3, tiles)):
                        dst = fbk[(M0 + n) % 3][:, (t - 3 * n) * MS:(t - 3 * n + 1) * MS]
                        pe.matmul(dst, ones_bf[:], bias_parts[:, 4 * P:4 * P + MS], start=True, stop=False)
                        last = pe.matmul(dst, hT[par][:, t * P:(t + 1) * P], w_ms[:], start=False, stop=True)
                    last.then_inc(front_done, 1)

            def turn_rows(g):
                pe.wait_ge(coord_ready, 3 * g + 1)
                pe.wait_ge(stage_ready, g + 1)
                for n in range(4):
                    last = pe.transpose(fbk[SR % 3][:, n * P:(n + 1) * P],
                                        stage[:, n // 2, n % 2].rearrange("p b r -> p (b r)"), ident[:])
                last.then_inc(front_done, 1)

            def graph_edges(it, par, g, b):
                pe.wait_ge(*((coord_ready, 3 * g + 2), (rows_ready, g + 1), (exp_ready, GB * g + 1),
                             (exp_ready, GB * g + 2))[b])
                pe.wait_ge(adj_in[b], 16 * (g + 1))
                bank = fbk[J[b] % 3]
                for mt in range(2):
                    for nt in range(2):
                        last = pe.transpose(bank[:, mt * nodes + nt * P:mt * nodes + (nt + 1) * P],
                                            adj_sb[:, b, nt, mt * P:(mt + 1) * P], ident[:])
                last.then_inc(front_done, 1)
                pe.wait_ge(*((coord_ready, 3 * g + 3), (edge_ready, GB * g + 1), (edge_ready, GB * g + 2),
                             (edge_ready, GB * g + 3))[b])
                pe.wait_ge(rows_ready, g + 1)
                mine = slice(SLOT * b, SLOT * b + KDIST)
                for mt in range(2):
                    last = pe.matmul(fbk[D[b] % 3][:, mt * nodes:(mt + 1) * nodes],
                                     rows[mine, mt * P:(mt + 1) * P], rows[mine, 2 * P:4 * P],
                                     start=True, stop=True)
                last.then_inc(front_done, 1)

            def gather(g, h):
                pe.wait_ge(*((exp_ready, GB * g + 3), (edge_ready, GB * g + 4))[h])
                pe.wait_ge(edge_ready, GB * g + 2 * h + 2)
                pe.wait_ge(msg_ready, 3 * g + 3)
                for b in (2 * h, 2 * h + 1):
                    for mt in range(2):
                        last = pe.matmul(fbk[(N0 + h) % 3][:, (b % 2) * nodes:(b % 2 + 1) * nodes],
                                         msg[:, 2 * b + mt, :], edge[:, b, mt, :], start=mt == 0,
                                         stop=mt == 1)
                last.then_inc(front_done, 1)

            def gate_tile(par, gb, t):
                wait(pe, q_ready, tiles * gb + t - 1)
                cols = slice(t * P, (t + 1) * P)
                bank = gbk[t % 2]
                pe.matmul(bank[:], ones_bf[:], bias_parts[:, 0:4 * P], start=True, stop=False)
                products(bank[:, P:4 * P], [(hT_hi[par][:, cols], hT_lo[par][:, cols],
                                             gate_hi[:, GH], gate_lo[:, GH])], False, False)
                if t == 0:
                    pe.wait_ge(nm_lo_ready, 2 * gb + 2)
                products(bank[:, 0:3 * P], [(nm_hi[:, cols], nm_lo[:, cols],
                                             gate_hi[:, GN], gate_lo[:, GN])], False, False)
                if t == 0:
                    pe.wait_ge(xc_hi_ready, gb + 1)
                    pe.wait_ge(xc_lo_ready, gb + 1)
                products(bank[:, 0:3 * P], [(xc_hi[:, cols], xc_lo[:, cols],
                                             gate_hi[:, GX], gate_lo[:, GX])], False, True)\
                    .then_inc(gate_done, 1)

            def step(it, par, front, back):
                g = 2 * it + par
                gb = g - 1
                if isinstance(it, int) and it == 0:
                    if par:
                        pe.wait_ge(filt_hi_ready, len(leaf_at))
                        pe.wait_ge(filt_lo_ready, len(leaf_at))
                    else:
                        pe.wait_ge(small_ready, 6)
                        pe.wait_ge(taps_v, 3)
                        pe.wait_ge(taps_a, 2)
                        pe.wait_ge(bias_link, BIAS_LINKS)
                if back:
                    pe.wait_ge(leaf_hi_ready, 2 * g)
                    pe.wait_ge(leaf_lo_ready, 2 * g)
                    conv(par, gb, CV_BB, B, (B,), y_ready, 2 * gb - 1)
                    conv(par, gb, CV_B, B, (A, C), p_copied, 3 * gb)
                    conv(par, gb, CV_AB, A, (B,), y_ready, 2 * gb)
                if front:
                    turn_nodes(par, g)
                if back:
                    conv(par, gb, CV_A, A, (A, C), p_copied, 3 * gb + 1)
                if front:
                    conv1(par, g)
                if back:
                    conv(par, gb, CV_CB, C, (B,), mb_ready, gb + 1)
                if front:
                    messages(par, g)
                if back:
                    conv(par, gb, CV_C, C, (A, C), p_copied, 3 * gb + 2)
                if front:
                    turn_rows(g)
                    graph_edges(it, par, g, 0)
                    graph_edges(it, par, g, 1)
                for t in range(tiles):
                    if back:
                        gate_tile(1 - par, gb, t)
                    if front and t in (2, 4):
                        graph_edges(it, par, g, 2 if t == 2 else 3)
                if front:
                    gather(g, 0)
                    gather(g, 1)

            steps(pe, step)


_INS = ["x", "adj"] + ["L0_gnn_" + n for n in (
    "w_se", "b_se", "conv1_w", "bn1_g", "bn1_b", "bn1_m", "bn1_v", "conv2_w", "bn2_g", "bn2_b", "bn2_m",
    "bn2_v", "w_msg", "b_msg", "w_ih", "b_ih", "w_hh", "b_hh")]


def kernel(**inputs):
    import numpy as np
    import concourse.bacc as bacc
    from concourse.bass_utils import run_bass_kernel_spmd

    nc = bacc.Bacc("TRN2", target_bir_lowering=False, num_devices=1)
    arrays, args = {}, []
    for name in _INS:
        a = np.ascontiguousarray(inputs[name])
        arrays[f"in_{name}"] = a
        args.append(nc.dram_tensor(f"in_{name}", a.shape, F32, kind="ExternalInput").ap())
    shape = arrays["in_x"].shape
    out = nc.dram_tensor("out_0", shape, F32, kind="ExternalOutput").ap()
    build(nc, *args, out)
    r = run_bass_kernel_spmd(nc, [arrays], core_ids=[0])
    return r.results[0]["out_0"]
```

```python
from contextlib import ExitStack

import concourse.bass as bass
from concourse import mybir

F32 = mybir.dt.float32
F32R = mybir.dt.float32r
BF16 = mybir.dt.bfloat16
ALU = mybir.AluOpType
ACT = mybir.ActivationFunctionType
AX = mybir.AxisListType

P = 128
GB = 4
EPS = 1e-5
TAPS = 17
HALO = TAPS // 2
LEAVES = 3
A, B, C = range(LEAVES)
MS = 132
SLOT = 32
ROWS = 5
KDIST = 4 * ROWS

(T0, T1, M0, M1, M2, C0, C1, SR, J0, D0, J1, D1, J2, D2, J3, D3, N0, N1) = range(18)
J = (J0, J1, J2, J3)
D = (D0, D1, D2, D3)
FRONT = 18
(CV_BB, CV_B, CV_AB, CV_A, CV_CB, CV_C) = range(6)
CONV = 6


def leaf_taps():
    even = {A: (TAPS + 1) // 2, B: (TAPS + 1) // 2, C: TAPS // 2}
    place, at = {}, 0
    for s in (A, B, C):
        for leaf in (A, B, C):
            n = even[s] // 2 if leaf == C else (even[s] + 1) // 2
            place[s, leaf] = (at, n)
            at += n
    return place, at


def build(nc, x, adj, w_se, b_se, conv1_w, bn1_g, bn1_b, bn1_m, bn1_v, conv2_w, bn2_g, bn2_b,
          bn2_m, bn2_v, w_msg, b_msg, w_ih, b_ih, w_hh, b_hh, out):
    graphs, nodes, feats = x.shape
    assert feats == P and nodes == 2 * P and graphs % (2 * GB) == 0
    groups = graphs // GB
    tiles = GB * nodes // P
    half_tiles = tiles // 2
    quarter = nodes // 4
    xw = (nodes + 2 * HALO) // 2
    lw = xw // 2
    leaf_at, n_filters = leaf_taps()
    SEC = GB * lw

    ctx = ExitStack()
    with ctx:
        def sb(name, shape, dt=F32):
            return ctx.enter_context(nc.sbuf_tensor(name, shape, dt))

        def sem(name):
            return ctx.enter_context(nc.semaphore(name))

        x_ring = sb("x_ring", [P, 4 * tiles * P])
        hn = [sb(f"hn{i}", [P, tiles, P]) for i in range(2)]
        hT = [sb(f"hT{i}", [P, tiles * P]) for i in range(2)]
        hT_hi = [sb(f"hT_hi{i}", [P, tiles * P], F32R) for i in range(2)]
        hT_lo = [sb(f"hT_lo{i}", [P, tiles * P], F32R) for i in range(2)]
        Xe = sb("Xe", [P, GB, xw])
        sect = sb("sect", [P, LEAVES, GB, xw])
        diff = sb("diff", [P, 2, LEAVES * GB, lw])
        leaf_hi = sb("leaf_hi", [P, LEAVES, LEAVES * GB, lw], F32R)
        leaf_lo = sb("leaf_lo", [P, LEAVES, LEAVES * GB, lw], F32R)
        LEAF_SLOT = {A: 0, C: 1, B: 2}
        filt_hi = sb("filt_hi", [P, n_filters, P], F32R)
        filt_lo = sb("filt_lo", [P, n_filters, P], F32R)
        c1_hi = sb("c1_hi", [P, P], F32R)
        c1_lo = sb("c1_lo", [P, P], F32R)
        w_ms = sb("w_ms", [P, MS])
        gate_hi = sb("gate_hi", [P, 3, 3 * P], F32R)
        gate_lo = sb("gate_lo", [P, 3, 3 * P], F32R)
        GX, GN, GH = range(3)
        ident = sb("ident", [P, P])
        ones_bf = sb("ones_bf", [P, P], BF16)
        BIAS_W = 4 * P + MS
        bias_parts = sb("bias_parts", [P, BIAS_W], BF16)
        scratch = sb("scratch", [P, 6400])
        xc_hi = sb("xc_hi", [P, tiles * P], F32R)
        xc_lo = sb("xc_lo", [P, tiles * P], F32R)
        nm_hi = sb("nm_hi", [P, tiles * P], F32R)
        nm_lo = sb("nm_lo", [P, tiles * P], F32R)
        adj_sb = sb("adj_sb", [P, GB, 2, nodes])
        edge = sb("edge", [P, GB, 2, nodes])
        msg = sb("msg", [P, tiles, P])
        stage = sb("stage", [P, 2, 2, GB, SLOT])
        rows = sb("rows", [P, 4 * P], F32R)
        stats = sb("stats", [P, tiles, 6])
        spread = sb("spread", [P, tiles])
        mean = sb("mean", [P, tiles])
        veps = sb("veps", [P, tiles])
        rstd = sb("rstd", [P, tiles])
        neg_half = sb("neg_half", [P, tiles])
        coord = sb("coord", [P, tiles, 3])
        coord2 = sb("coord2", [P, tiles, 3])
        dist_f = sb("dist_f", [P, 2, 2, GB, ROWS])
        bn = sb("bn", [P, 2, 4])
        bn_s = sb("bn_s", [P, 4, 2])

        off = 0

        def carve(n):
            nonlocal off
            off += n
            return scratch[:, off - n:off]
        rz = carve(tiles * 2 * P).rearrange("p (t c) -> p t c", t=tiles)
        q = carve(tiles * P).rearrange("p (t c) -> p t c", t=tiles)
        dd = carve(tiles * P).rearrange("p (t c) -> p t c", t=tiles)
        ysum = carve(tiles * P)
        pcopy = carve(3 * GB * quarter).rearrange("p (s c) -> p s c", s=3)
        m_b = carve(2 * GB * quarter)
        off = 0
        raw2 = carve(TAPS * P)
        w2T = carve(TAPS * P).rearrange("p (k o) -> p k o", k=TAPS)
        fb = carve((TAPS + 1) // 2 * P).rearrange("p (k o) -> p k o", o=P)
        fsum = raw2[:, 0:14 * P].rearrange("p (k o) -> p k o", o=P)
        edge_flat = edge[:].rearrange("p b t n -> p (b t n)")
        raw_ih = edge_flat[:, 0:6 * P].rearrange("p (g c) -> p g c", g=3)
        raw_hh = edge_flat[:, 6 * P:9 * P].rearrange("p (g c) -> p g c", g=3)
        raw_c1 = edge_flat[:, 9 * P:10 * P]
        raw_msg = edge_flat[:, 10 * P:11 * P]
        raw_se = edge_flat[0:3, 11 * P:12 * P]
        row0 = msg[0:1, :, :].rearrange("p t c -> p (t c)")
        bias_row = row0[:, 0:BIAS_W]
        bhh_row = sb("bhh_row", [1, 3 * P])
        part_row = sb("part_row", [1, BIAS_W], BF16)

        cb = [ctx.enter_context(nc.psum_tensor(f"conv_bank{i}", [P, 512], F32)) for i in range(3)]
        gbk = [ctx.enter_context(nc.psum_tensor(f"gate_bank{i}", [P, 512], F32)) for i in range(2)]
        fbk = [ctx.enter_context(nc.psum_tensor(f"front_bank{i}", [P, 512], F32)) for i in range(3)]

        x_in = [sem(f"x_in{i}") for i in range(2)]
        adj_in = [sem(f"adj_in{b}") for b in range(GB)]
        out_stored = [sem(f"out_stored{h}") for h in range(2)]
        front_done = sem("front_done")
        conv_done = sem("conv_done")
        gate_done = sem("gate_done")
        hT_ready = sem("hT_ready")
        h1_ready = sem("h1_ready")
        p_copied = sem("p_copied")
        msg_ready = sem("msg_ready")
        rows_ready = sem("rows_ready")
        exp_ready = sem("exp_ready")
        xc_hi_ready = sem("xc_hi_ready")
        leaf_hi_ready = sem("leaf_hi_ready")
        rz_ready = sem("rz_ready")
        n_ready = sem("n_ready")
        nm_hi_ready = sem("nm_hi_ready")
        ln_link = sem("ln_link")
        veps_ready = sem("veps_ready")
        hn_ready = sem("hn_ready")
        hT_split = sem("hT_split")
        mb_ready = sem("mb_ready")
        y_ready = sem("y_ready")
        coord_ready = sem("coord_ready")
        row_link = sem("row_link")
        stage_ready = sem("stage_ready")
        edge_ready = sem("edge_ready")
        xc_lo_ready = sem("xc_lo_ready")
        leaf_lo_ready = sem("leaf_lo_ready")
        m_ready = sem("m_ready")
        q_ready = sem("q_ready")
        d_ready = sem("d_ready")
        out_ready = sem("out_ready")
        nm_lo_ready = sem("nm_lo_ready")
        rstd_ready = sem("rstd_ready")
        q_res = sem("q_res")
        diff_ready = sem("diff_ready")
        p_ready = sem("p_ready")
        ident_ready = sem("ident_ready")
        pool_link = sem("pool_link")
        zero_ready = sem("zero_ready")
        bn_in = sem("bn_in")
        w_in = sem("w_in")
        bias_in = sem("bias_in")
        w2_in = sem("w2_in")
        bn_veps = sem("bn_veps")
        bn_powed = sem("bn_powed")
        bn_ready = sem("bn_ready")
        raw_scaled = sem("raw_scaled")
        w_turned = sem("w_turned")
        c1_ready = sem("c1_ready")
        ms_ready = sem("ms_ready")
        taps_copied = sem("taps_copied")
        tap_sums = sem("tap_sums")
        filt_hi_ready = sem("filt_hi_ready")
        filt_lo_ready = sem("filt_lo_ready")
        gate_hi_ready = sem("gate_hi_ready")
        gate_lo_ready = sem("gate_lo_ready")
        bias_set = sem("bias_set")
        part_cut = sem("part_cut")
        part_placed = sem("part_placed")
        part_left = sem("part_left")

        block = ctx.enter_context(nc.Block())

        def wait(eng, s, value):
            if not isinstance(value, int) or value > 0:
                eng.wait_ge(s, value)

        def steps(eng, step):
            step(0, 0, True, False)
            step(0, 1, True, True)
            with eng.Fori(1, groups // 2) as it:
                for par in range(2):
                    step(it, par, True, True)
            step(groups // 2, 0, False, True)

        def slot(it, par):
            return ((it % 2) * 2 + par) * (tiles * P)

        def slot_before(it, par):
            return slot(it, 0) if par else (((it + 1) % 2) * 2 + 1) * (tiles * P)

        ZEROS = 11
        LINKS, NORM_LINKS = 7, 7
        W_SMALL, W_TAPS, W_GATES = 1, 6, 9
        SUM_AT = {A: 0, B: 5, C: 10}

        def phases(ap, l1):
            return ap.rearrange("p (b i l m) -> p l b i m", b=GB, i=quarter, l=2)[:, :, :, :, l1]

        def by_phase(ap):
            return ap.rearrange("p (l b i) -> p l b i", l=2, b=GB)

        def for_both(ap):
            return ap.rearrange("p (l b i) -> p l b i", l=1, b=GB).broadcast_to([P, 2, GB, quarter])

        def half_of(ap, h):
            return ap[:, h * half_tiles:(h + 1) * half_tiles, :].rearrange("p t c -> p (t c)")

        def ms_bank(n, nt):
            return fbk[(M0 + n) % 3][:, 0:nt * MS].rearrange("p (t c) -> p t c", c=MS)

        samples = sect[:].rearrange("p s b n -> p (s b) n")

        def half_run(s, first, n):
            if s == B:
                return fb[:, first:first + 2 * n - 1:2, :]
            k = 2 * first + (s == C)
            return w2T[:, k:k + 4 * n - 3:4, :]

        def leaf_source(s, leaf):
            n = leaf_at[s, leaf][1]
            if leaf == A:
                return half_run(s, 0, n)
            if leaf == C:
                return half_run(s, 1, n)
            return fsum[:, SUM_AT[s]:SUM_AT[s] + n, :]

        @block.sync
        def _(sp):
            def load_x(it, par, g):
                at = slot(it, par)
                sp.dma_start(x_ring[:, bass.ds(at, tiles * P)].rearrange("p (b t c) -> p b t c", b=GB, t=2),
                             x_groups[g]).then_inc(x_in[par], 16)

            x_groups = x.rearrange("(g b) (t p) c -> g p b t c", b=GB, p=P)
            o_groups = out.rearrange("(g b) (t p) c -> g p b t c", b=GB, p=P)
            a_graphs = adj.rearrange("(g b) (t p) m -> g b p t m", b=GB, p=P)

            def step(it, par, front, back, load):
                g = 2 * it + par
                at = slot_before(it, par)
                if front:
                    for b in range(GB):
                        wait(sp, front_done, FRONT * (g - 1) + J[b] + 1)
                        sp.dma_start(adj_sb[:, b, :, :], a_graphs[g, b]).then_inc(adj_in[b], 16)
                if back:
                    for h in range(2):
                        wait(sp, out_stored[h], 16 * (g - 1))
                if load:
                    sp.wait_ge(hn_ready, 2 * g + 2)
                    load_x(it + 1, par, g + 2)
                if back:
                    for h in range(2):
                        sp.wait_ge(out_ready, 2 * (g - 1) + h + 1)
                        half = GB // 2
                        sp.dma_start(
                            o_groups[g - 1][:, half * h:half * h + half],
                            x_ring[:, bass.ds(at + h * half_tiles * P, half_tiles * P)]
                            .rearrange("p (b t c) -> p b t c", b=half, t=2),
                        ).then_inc(out_stored[h], 16)

            load_x(0, 0, 0)
            sp.dma_start(raw2, conv2_w.rearrange("o i k -> o (i k)")).then_inc(w2_in, 16)
            load_x(0, 1, 1)
            step(0, 0, True, False, True)
            step(0, 1, True, True, True)
            with sp.Fori(1, groups // 2 - 1) as it:
                for par in range(2):
                    step(it, par, True, True, True)
            step(groups // 2 - 1, 0, True, True, False)
            step(groups // 2 - 1, 1, True, True, False)
            step(groups // 2, 0, False, True, False)
            for h in range(2):
                sp.wait_ge(out_stored[h], 16 * groups)

        @block.gpsimd
        def _(pool):
            pool.memset(ident[:], 0.0).then_inc(pool_link, 1)
            pool.wait_ge(pool_link, 1)
            pool.affine_select(out=ident[:], in_=ident[:], compare_op=ALU.not_equal, fill=1.0, base=0,
                               pattern=[[-1, P]], channel_multiplier=1).then_inc(ident_ready, 1)
            pad, end = HALO // 2, HALO // 2 + nodes // 2
            pool.memset(neg_half[:], -0.5).then_inc(zero_ready, 1)
            for v in (Xe[:], sect[:, B]):
                pool.memset(v[:, :, 0:pad], 0.0).then_inc(zero_ready, 1)
                pool.memset(v[:, :, end:xw], 0.0).then_inc(zero_ready, 1)
            pool.memset(sect[:, C, :, xw - 1:xw], 0.0).then_inc(zero_ready, 1)
            pool.memset(diff[:, 1, :, lw - 1:lw], 0.0).then_inc(zero_ready, 1)
            pool.memset(stage[:], 0.0).then_inc(zero_ready, 1)
            pool.memset(dist_f[:, 0, :, :, 3:4], -1.0).then_inc(zero_ready, 1)
            pool.memset(dist_f[:, 1, :, :, 4:5], 1.0).then_inc(zero_ready, 1)
            pool.memset(ones_bf[:], 1.0).then_inc(zero_ready, 1)
            pool.memset(bias_parts[:], 0.0).then_inc(part_placed, 1)
            pool.wait_ge(zero_ready, ZEROS)
            pool.wait_ge(bn_veps, 1)
            pool.tensor_tensor(bn_s[:, 1], bn_s[:, 0], neg_half[:, 0:2], ALU.pow).then_inc(bn_powed, 1)

            def step(it, par, front, back):
                g = 2 * it + par
                gb = g - 1
                if front:
                    pool.wait_ge(veps_ready, g + 1)
                    wait(pool, hn_ready, 2 * g)
                    pool.tensor_tensor(rstd[:], veps[:], neg_half[:], ALU.pow).then_inc(rstd_ready, 1)
                if back:
                    pool.wait_ge(mb_ready, gb + 1)
                    wait(pool, xc_hi_ready, gb)
                    wait(pool, xc_lo_ready, gb)
                    for l1 in range(2):
                        pool.tensor_tensor(phases(ysum, l1), phases(hT[1 - par][:], l1), by_phase(m_b),
                                           ALU.add).then_inc(q_res, 1)
                    pool.wait_ge(p_copied, 3 * gb + 2)
                    pool.wait_ge(q_res, 4 * gb + 1)
                    pool.tensor_tensor(phases(ysum, 0), phases(ysum, 0), for_both(pcopy[:, 1, :]),
                                       ALU.add).then_inc(q_res, 1)
                    pool.wait_ge(p_copied, 3 * gb + 3)
                    pool.wait_ge(q_res, 4 * gb + 2)
                    pool.tensor_tensor(phases(ysum, 1), phases(ysum, 1), for_both(pcopy[:, 2, :]),
                                       ALU.add).then_inc(q_res, 1)
                if front:
                    pool.wait_ge(h1_ready, 4 * g + 4)
                    pool.tensor_tensor(sect[:, A], Xe[:], sect[:, B], ALU.subtract).then_inc(diff_ready, 1)
                    pool.tensor_tensor(sect[:, C, :, 0:xw - 1], Xe[:, :, 1:xw], sect[:, B, :, 0:xw - 1],
                                       ALU.subtract).then_inc(diff_ready, 1)
                if front:
                    pool.wait_ge(diff_ready, 4 * g + 2)
                    wait(pool, leaf_hi_ready, 2 * g)
                    wait(pool, leaf_lo_ready, 2 * g)
                    pool.tensor_tensor(diff[:, 0], samples[:, :, 0:xw:2], samples[:, :, 1:xw:2],
                                       ALU.subtract).then_inc(diff_ready, 1)
                    pool.tensor_tensor(diff[:, 1, :, 0:lw - 1], samples[:, :, 2:xw:2],
                                       samples[:, :, 1:xw - 2:2], ALU.subtract).then_inc(diff_ready, 1)
                if back:
                    at = slot_before(it, par)
                    for h in range(2):
                        pool.wait_ge(n_ready, 2 * gb + h + 1)
                        part = x_ring[:, bass.ds(at + h * half_tiles * P, half_tiles * P)]
                        pool.tensor_tensor(part, part, half_of(q, h), ALU.add).then_inc(p_ready, 1)

            steps(pool, step)

        @block.scalar
        def _(act):
            def row(vec):
                return vec.rearrange("(a n) -> a n", a=1)

            def column(vec):
                return vec.rearrange("(p a) -> p a", a=1)

            act.dma_start(raw_c1, conv1_w.rearrange("o i k -> o (i k)")).then_inc(bn_in, 16)
            for n, vecs in enumerate(((bn1_v, bn1_g, bn1_b, bn1_m), (bn2_v, bn2_g, bn2_b, bn2_m))):
                for k, vec in enumerate(vecs):
                    act.dma_start(bn[:, n, k:k + 1], column(vec)).then_inc(bn_in, 16)
            act.dma_start(raw_msg, w_msg).then_inc(w_in, 16)
            act.dma_start(raw_se, w_se).then_inc(w_in, 16)
            for dst, src in ((bias_row[:, 0:P], b_ih[2 * P:3 * P]), (bias_row[:, P:3 * P], b_ih[0:2 * P]),
                             (bias_row[:, 4 * P:5 * P], b_msg), (bias_row[:, 5 * P:5 * P + 3], b_se),
                             (bhh_row[:], b_hh)):
                act.dma_start(dst, row(src)).then_inc(bias_in, 16)
            act.dma_start(raw_hh, w_hh.rearrange("(g o) c -> o g c", g=3)).then_inc(w_in, 16)
            act.dma_start(raw_ih, w_ih.rearrange("(g o) c -> o g c", g=3)).then_inc(w_in, 16)

            def conv1_hi():
                act.wait_ge(w_turned, W_SMALL)
                act.activation(c1_hi[:], gbk[0][:, 0:P], ACT.Copy).then_inc(c1_ready, 1)

            def taps():
                act.wait_ge(w_turned, 2)
                act.wait_ge(ms_ready, 2)
                act.activation(w2T[:, TAPS - 1, :], gbk[0][:, 3 * P:4 * P], ACT.Copy).then_inc(taps_copied, 1)
                for n, bank in enumerate((gbk[1], cb[0], cb[1], cb[2])):
                    act.wait_ge(w_turned, 3 + n)
                    act.activation(w2T[:, 4 * n:4 * n + 4, :].rearrange("p k o -> p (k o)"), bank[:],
                                   ACT.Copy).then_inc(taps_copied, 1)

            def cut_bias():
                act.wait_ge(part_placed, 1)
                for k in range(3):
                    act.wait_ge(*((part_left, k) if k else (bias_set, 3)))
                    if k:
                        act.wait_ge(part_placed, k + 1)
                    act.activation(part_row[:], bias_row, ACT.Copy).then_inc(part_cut, 1)
                    act.wait_ge(part_cut, k + 1)
                    act.activation(bias_parts[32 * k:32 * k + 1, :], part_row[:],
                                   ACT.Copy).then_inc(part_placed, 1)

            def filters_hi():
                act.wait_ge(tap_sums, 5)
                for key in sorted(leaf_at):
                    at, k = leaf_at[key]
                    act.activation(filt_hi[:, at:at + k, :], leaf_source(*key), ACT.Copy)\
                       .then_inc(filt_hi_ready, 1)

            def gates_hi():
                for n in range(3):
                    act.wait_ge(w_turned, W_TAPS + n + 1)
                    act.activation(gate_hi[:, n], cb[n][:, 0:3 * P], ACT.Copy).then_inc(gate_hi_ready, 1)

            def edges(g, b):
                act.wait_ge(front_done, FRONT * g + D[b] + 1)
                act.activation(edge[:, b].rearrange("p t n -> p (t n)"), fbk[D[b] % 3][:],
                               ACT.Exp).then_inc(exp_ready, 1)

            def shared(gb, n, kind):
                act.wait_ge(conv_done, CONV * gb + kind + 1)
                if n == 0:
                    wait(act, mb_ready, gb)
                    act.activation(pcopy[:, 0, :], cb[kind % 3][:, 0:GB * quarter], ACT.Identity,
                                   bias=bn_s[:, 3, 1:2]).then_inc(p_copied, 1)
                else:
                    wait(act, q_res, 4 * gb)
                    act.activation(pcopy[:, n, :], cb[kind % 3][:, 0:GB * quarter],
                                   ACT.Copy).then_inc(p_copied, 1)

            def step(it, par, front, back):
                g = 2 * it + par
                gb = g - 1
                first = isinstance(it, int) and it == 0 and par == 0
                if back:
                    shared(gb, 0, CV_BB)
                    shared(gb, 1, CV_AB)
                if first:
                    conv1_hi()
                if front:
                    wait(act, front_done, FRONT * (g - 2) + M2 + 1)
                    wait(act, hT_split, 4 * (g - 1))
                    wait(act, q_res, 4 * (g - 1))
                    for h in range(2):
                        act.wait_ge(front_done, FRONT * g + T0 + h + 1)
                        act.activation(hT[par][:, h * 512:(h + 1) * 512], fbk[(T0 + h) % 3][:],
                                       ACT.Relu).then_inc(hT_ready, 1)
                if back:
                    shared(gb, 2, CV_CB)
                if first:
                    taps()
                    cut_bias()
                if front:
                    wait(act, front_done, FRONT * g)
                    if first:
                        act.wait_ge(part_left, 3)
                    for n in range(3):
                        act.wait_ge(front_done, FRONT * g + M0 + n + 1)
                        nt = min(3, tiles - 3 * n)
                        act.activation(msg[:, 3 * n:3 * n + nt, :], ms_bank(n, nt)[:, :, 0:P],
                                       ACT.Relu).then_inc(msg_ready, 1)
                    wait(act, diff_ready, 4 * g)
                    wait(act, leaf_lo_ready, 2 * g)
                    wait(act, leaf_hi_ready, 2 * g)
                    if first:
                        act.wait_ge(bn_ready, 3)
                        act.wait_ge(zero_ready, ZEROS)
                    for h in range(2):
                        act.wait_ge(front_done, FRONT * g + C0 + h + 1)
                        v = fbk[(C0 + h) % 3][:].rearrange("p (b n m) -> p b n m", b=2, m=2)
                        pad = HALO // 2
                        for m, dst in ((0, Xe[:, 2 * h:2 * h + 2]), (1, sect[:, B, 2 * h:2 * h + 2])):
                            act.activation(dst[:, :, pad:pad + nodes // 2], v[:, :, :, m], ACT.Relu,
                                           bias=bn_s[:, 3, 0:1]).then_inc(h1_ready, 1)
                    if first:
                        filters_hi()
                        gates_hi()
                    act.wait_ge(front_done, FRONT * g + SR + 1)
                    act.activation(rows[:], fbk[SR % 3][:], ACT.Copy).then_inc(rows_ready, 1)
                    edges(g, 0)
                if back:
                    wait(act, gate_done, tiles * gb)
                    act.wait_ge(y_ready, 2 * gb + 2)
                    act.activation(xc_hi[:], ysum, ACT.Relu).then_inc(xc_hi_ready, 1)
                if front:
                    edges(g, 1)
                for t in range(tiles):
                    if back:
                        act.wait_ge(gate_done, tiles * gb + t + 1)
                        if t == 0:
                            wait(act, d_ready, 4 * gb)
                        act.activation(rz[:, t, :], gbk[t % 2][:, P:3 * P], ACT.Tanh,
                                       scale=0.5).then_inc(rz_ready, 1)
                    if front and t in (3, 5):
                        edges(g, 2 if t == 3 else 3)
                    if front and t == 2:
                        wait(act, conv_done, CONV * g)
                        act.wait_ge(diff_ready, 4 * g + 4)
                        act.activation(leaf_hi[:, 0:2], diff[:], ACT.Copy).then_inc(leaf_hi_ready, 1)
                        act.activation(leaf_hi[:, 2], samples[:, :, 1:xw:2],
                                       ACT.Copy).then_inc(leaf_hi_ready, 1)
                    if back and t == 5:
                        new_state(gb, 0)
                if back:
                    new_state(gb, 1)
                if front:
                    wait(act, gate_done, tiles * g)
                    for h in range(2):
                        act.wait_ge(front_done, FRONT * g + N0 + h + 1)
                        act.activation(nm_hi[:, h * 512:(h + 1) * 512], fbk[(N0 + h) % 3][:],
                                       ACT.Copy).then_inc(nm_hi_ready, 1)

            def new_state(gb, h):
                act.wait_ge(q_ready, tiles * gb + half_tiles * (h + 1))
                act.activation(half_of(q, h), half_of(q, h), ACT.Tanh).then_inc(n_ready, 1)

            steps(act, step)

        @block.vector
        def _(dve):
            def lo_part(out_ap, src, hi):
                return dve.tensor_tensor(out_ap, src, hi.bitcast(F32), ALU.subtract)

            def batch_norms():
                dve.wait_ge(bn_powed, 1)
                dve.tensor_tensor(bn_s[:, 2], bn[:, :, 1], bn_s[:, 1], ALU.mult).then_inc(bn_ready, 1)
                dve.wait_ge(bn_ready, 1)
                dve.tensor_scalar(raw_c1, raw_c1, bn_s[:, 2, 0:1], None, ALU.mult).then_inc(raw_scaled, 1)
                dve.tensor_tensor(bn_s[:, 3], bn[:, :, 3], bn_s[:, 2], ALU.mult).then_inc(bn_ready, 1)
                dve.wait_ge(bn_ready, 2)
                dve.tensor_tensor(bn_s[:, 3], bn[:, :, 2], bn_s[:, 3], ALU.subtract).then_inc(bn_ready, 1)

            def scale_conv2():
                dve.wait_ge(w2_in, 16)
                dve.tensor_scalar(raw2, raw2, bn_s[:, 2, 1:2], None, ALU.mult).then_inc(raw_scaled, 1)

            def small_weights():
                dve.wait_ge(c1_ready, 1)
                lo_part(c1_lo[:], gbk[0][:, 0:P], c1_hi[:]).then_inc(c1_ready, 1)
                dve.memset(w_ms[:, MS - 1:MS], 0.0).then_inc(ms_ready, 1)
                dve.tensor_copy(w_ms[:, 0:MS - 1], gbk[0][:, P:P + MS - 1]).then_inc(ms_ready, 1)

            def bias_rows():
                dve.wait_ge(bias_in, 16 * 5)
                dve.memset(bias_row[:, BIAS_W - 1:BIAS_W], 0.0).then_inc(bias_set, 1)
                dve.tensor_tensor(bias_row[:, P:3 * P], bias_row[:, P:3 * P], bhh_row[:, 0:2 * P],
                                  ALU.add).then_inc(bias_set, 1)
                dve.tensor_scalar(bias_row[:, 3 * P:4 * P], bhh_row[:, 2 * P:3 * P], 0.5, None,
                                  ALU.mult).then_inc(bias_set, 1)
                dve.wait_ge(w_in, 16 * 4)
                dve.tensor_scalar(raw_hh[:, 2, :], raw_hh[:, 2, :], 0.5, None,
                                  ALU.mult).then_inc(raw_scaled, 1)

            def bias_left():
                for k in range(3):
                    dve.wait_ge(part_cut, k + 1)
                    if k == 0:
                        dve.wait_ge(bias_set, 3)
                    else:
                        dve.wait_ge(part_left, k)
                    dve.tensor_tensor(bias_row, bias_row, part_row[:], ALU.subtract).then_inc(part_left, 1)

            def sum_taps():
                dve.wait_ge(taps_copied, 5)
                dve.tensor_tensor(fb[:, 0:TAPS // 2, :], w2T[:, 0:TAPS - 1:2, :], w2T[:, 1:TAPS:2, :],
                                  ALU.add).then_inc(tap_sums, 1)
                dve.tensor_copy(fb[:, TAPS // 2, :], w2T[:, TAPS - 1, :]).then_inc(tap_sums, 1)
                dve.wait_ge(tap_sums, 2)
                for s in (A, B, C):
                    n_even, n_odd = leaf_at[s, A][1], leaf_at[s, C][1]
                    if n_even > n_odd:
                        dve.tensor_copy(fsum[:, SUM_AT[s] + n_odd, :], half_run(s, 0, n_even)[:, n_odd, :])
                    dve.tensor_tensor(fsum[:, SUM_AT[s]:SUM_AT[s] + n_odd, :], half_run(s, 0, n_odd),
                                      half_run(s, 1, n_odd), ALU.add).then_inc(tap_sums, 1)

            def filters_lo():
                dve.wait_ge(tap_sums, 5)
                for n, key in enumerate(sorted(leaf_at)):
                    at, k = leaf_at[key]
                    dve.wait_ge(filt_hi_ready, n + 1)
                    lo_part(filt_lo[:, at:at + k, :], leaf_source(*key),
                            filt_hi[:, at:at + k, :]).then_inc(filt_lo_ready, 1)

            def gates_lo():
                for n in range(3):
                    dve.wait_ge(gate_hi_ready, n + 1)
                    lo_part(gate_lo[:, n], cb[n][:, 0:3 * P], gate_hi[:, n]).then_inc(gate_lo_ready, 1)

            def norm_stats(it, par, g):
                dve.wait_ge(x_in[par], 16 * (it + 1))
                at = slot(it, par)
                for t in range(tiles):
                    last = dve.bn_stats(stats[:, t, :], x_ring[:, bass.ds(at + t * P, P)])
                last.then_inc(ln_link, 1)
                mean_e, m2_e, mean_o, m2_o = (stats[:, :, k] for k in (1, 2, 4, 5))
                dve.wait_ge(ln_link, NORM_LINKS * g + 1)
                dve.tensor_tensor(spread[:], mean_e, mean_o, ALU.subtract).then_inc(ln_link, 1)
                dve.tensor_tensor(mean[:], mean_e, mean_o, ALU.add).then_inc(ln_link, 1)
                dve.tensor_tensor(veps[:], m2_e, m2_o, ALU.add).then_inc(ln_link, 1)
                dve.wait_ge(ln_link, NORM_LINKS * g + 4)
                dve.tensor_tensor(spread[:], spread[:], spread[:], ALU.mult).then_inc(ln_link, 1)
                dve.tensor_scalar(mean[:], mean[:], 0.5, None, ALU.mult).then_inc(ln_link, 1)
                dve.tensor_scalar(veps[:], veps[:], 1.0 / P, EPS, ALU.mult, ALU.add).then_inc(ln_link, 1)
                dve.wait_ge(ln_link, NORM_LINKS * g + 7)
                dve.scalar_tensor_tensor(veps[:], spread[:], 0.25, veps[:], ALU.mult,
                                         ALU.add).then_inc(veps_ready, 1)

            def normalise(it, par, g):
                dve.wait_ge(rstd_ready, g + 1)
                wait(dve, front_done, FRONT * (g - 2) + T1 + 1)
                at = slot(it, par)
                for t in range(tiles):
                    last = dve.tensor_scalar(hn[par][:, t, :], x_ring[:, bass.ds(at + t * P, P)],
                                             mean[:, t:t + 1], rstd[:, t:t + 1], ALU.subtract, ALU.mult)
                    if t % half_tiles == half_tiles - 1:
                        last.then_inc(hn_ready, 1)

            def split_nodes(par, g):
                wait(dve, gate_done, tiles * (g - 1))
                for h in range(2):
                    cols = slice(h * 512, (h + 1) * 512)
                    dve.wait_ge(hT_ready, 2 * g + h + 1)
                    dve.tensor_copy(hT_hi[par][:, cols], hT[par][:, cols]).then_inc(hT_split, 1)
                    dve.wait_ge(hT_split, 4 * g + 2 * h + 1)
                    lo_part(hT_lo[par][:, cols], hT[par][:, cols], hT_hi[par][:, cols])\
                        .then_inc(hT_split, 1)

            def section_b(gb):
                dve.wait_ge(conv_done, CONV * gb + CV_B + 1)
                dve.wait_ge(p_copied, 3 * gb + 1)
                wait(dve, q_res, 4 * gb)
                dve.tensor_tensor(m_b.rearrange("p (l c) -> p l c", l=2),
                                  cb[CV_B % 3][:].rearrange("p (l c) -> p l c", l=2),
                                  pcopy[:, 0:1, :].broadcast_to([P, 2, GB * quarter]),
                                  ALU.add).then_inc(mb_ready, 1)

            def outputs(gb, l1):
                kind = (CV_A, CV_C)[l1]
                dve.wait_ge(conv_done, CONV * gb + kind + 1)
                dve.wait_ge(q_res, 4 * gb + 3 + l1)
                dve.tensor_tensor(phases(ysum, l1), by_phase(cb[kind % 3][:]), phases(ysum, l1),
                                  ALU.add).then_inc(y_ready, 1)

            def distance_rows(g):
                for n in range(3):
                    nt = min(3, tiles - 3 * n)
                    dve.wait_ge(msg_ready, 3 * g + n + 1)
                    dve.tensor_copy(coord[:, 3 * n:3 * n + nt, :],
                                    ms_bank(n, nt)[:, :, P:P + 3]).then_inc(coord_ready, 1)
                dve.wait_ge(coord_ready, 3 * g + 3)
                turned = coord[:].rearrange("p (b t) c -> p t b c", t=2)
                links = LINKS * g
                dve.tensor_tensor(coord2[:], coord[:], coord[:], ALU.mult).then_inc(row_link, 1)
                dve.tensor_scalar(dist_f[:, 0, :, :, 0:3], turned, 2.0, None, ALU.mult).then_inc(row_link, 1)
                dve.tensor_copy(dist_f[:, 1, :, :, 0:3], turned).then_inc(row_link, 1)
                dve.wait_ge(row_link, links + 3)
                dve.reduce_sum(dist_f[:, 1, :, :, 3], coord2[:].rearrange("p (b t) c -> p t b c", t=2),
                               axis=AX.X).then_inc(row_link, 1)
                dve.wait_ge(row_link, links + 4)
                dve.tensor_scalar(dist_f[:, 0, :, :, 4], dist_f[:, 1, :, :, 3], -1.0, None,
                                  ALU.mult).then_inc(row_link, 1)
                dve.wait_ge(row_link, links + 5)
                wait(dve, front_done, FRONT * (g - 1) + SR + 1)
                f = dist_f[:].rearrange("p s t b r -> p (s t b) r")
                st = stage[:].rearrange("p s t b r -> p (s t b) r")
                dve.tensor_copy(st[:, :, 0:ROWS].bitcast(F32R), f).then_inc(row_link, 1)
                dve.wait_ge(row_link, links + 6)
                dve.tensor_tensor(st[:, :, 3 * ROWS:4 * ROWS], f, st[:, :, 0:ROWS],
                                  ALU.subtract).then_inc(row_link, 1)
                dve.wait_ge(row_link, links + 7)
                half = 2 * GB
                for side, dst, src in ((0, 1, 0), (0, 2, 3), (1, 2, 0), (1, 1, 3)):
                    v = st[:, side * half:(side + 1) * half, :]
                    last = dve.tensor_copy(v[:, :, dst * ROWS:(dst + 1) * ROWS],
                                           v[:, :, src * ROWS:(src + 1) * ROWS])
                last.then_inc(stage_ready, 1)

            def edge_weights(g, b):
                dve.wait_ge(exp_ready, GB * g + b + 1)
                dve.wait_ge(front_done, FRONT * g + J[b] + 1)
                v = edge[:, b].rearrange("p t n -> p (t n)")
                dve.tensor_tensor(v, fbk[J[b] % 3][:], v, ALU.mult).then_inc(edge_ready, 1)

            def split_leaves(g):
                wait(dve, conv_done, CONV * g)
                dve.wait_ge(leaf_hi_ready, 2 * g + 1)
                lo_part(leaf_lo[:, 0:2], diff[:], leaf_hi[:, 0:2]).then_inc(leaf_lo_ready, 1)
                dve.wait_ge(leaf_hi_ready, 2 * g + 2)
                lo_part(leaf_lo[:, 2], samples[:, :, 1:xw:2], leaf_hi[:, 2]).then_inc(leaf_lo_ready, 1)

            def gates(gb, t):
                n = tiles * gb + t + 1
                dve.wait_ge(rz_ready, n)
                if t == 0:
                    wait(dve, p_ready, 2 * gb)
                dve.scalar_tensor_tensor(q[:, t, :], rz[:, t, 0:P], 1.0, gbk[t % 2][:, 3 * P:4 * P],
                                         ALU.add, ALU.mult).then_inc(m_ready, 1)
                dve.wait_ge(m_ready, n)
                dve.tensor_tensor(q[:, t, :], q[:, t, :], gbk[t % 2][:, 0:P], ALU.add).then_inc(q_ready, 1)

            def finish(it, par, gb, h):
                ts = slice(h * half_tiles, (h + 1) * half_tiles)
                dve.wait_ge(n_ready, 2 * gb + h + 1)
                dve.scalar_tensor_tensor(dd[:, ts, :], hn[1 - par][:, ts, :], 0.0, q[:, ts, :],
                                         ALU.max, ALU.subtract).then_inc(d_ready, 1)
                dve.wait_ge(d_ready, 4 * gb + 2 * h + 1)
                dve.scalar_tensor_tensor(dd[:, ts, :], rz[:, ts, P:2 * P], 1.0, dd[:, ts, :],
                                         ALU.add, ALU.mult).then_inc(d_ready, 1)
                dve.wait_ge(d_ready, 4 * gb + 2 * h + 2)
                dve.wait_ge(p_ready, 2 * gb + h + 1)
                part = x_ring[:, bass.ds(slot_before(it, par) + h * half_tiles * P, half_tiles * P)]
                dve.scalar_tensor_tensor(part, half_of(dd, h), 0.5, part, ALU.mult,
                                         ALU.add).then_inc(out_ready, 1)

            def step(it, par, front, back):
                g = 2 * it + par
                gb = g - 1
                first = isinstance(it, int) and it == 0 and par == 0
                if first:
                    dve.wait_ge(bn_in, 16 * 9)
                    dve.tensor_scalar(bn_s[:, 0], bn[:, :, 0], EPS, None, ALU.add).then_inc(bn_veps, 1)
                if front:
                    norm_stats(it, par, g)
                if first:
                    batch_norms()
                if back:
                    section_b(gb)
                if front:
                    normalise(it, par, g)
                if first:
                    scale_conv2()
                    small_weights()
                if back:
                    outputs(gb, 0)
                if front:
                    split_nodes(par, g)
                if first:
                    bias_rows()
                    bias_left()
                    sum_taps()
                if front:
                    distance_rows(g)
                if first:
                    filters_lo()
                    gates_lo()
                if back:
                    outputs(gb, 1)
                if front:
                    edge_weights(g, 0)
                if back:
                    wait(dve, gate_done, tiles * gb)
                    dve.wait_ge(xc_hi_ready, gb + 1)
                    dve.scalar_tensor_tensor(xc_lo[:], ysum, 0.0, xc_hi[:].bitcast(F32), ALU.max,
                                             ALU.subtract).then_inc(xc_lo_ready, 1)
                if front:
                    edge_weights(g, 1)
                for t in range(tiles):
                    if back:
                        gates(gb, t)
                    if front and t in (3, 5):
                        edge_weights(g, 2 if t == 3 else 3)
                    if front and t == 2:
                        split_leaves(g)
                    if back and t == 6:
                        finish(it, par, gb, 0)
                if back:
                    finish(it, par, gb, 1)
                if front:
                    for h in range(2):
                        cols = slice(h * 512, (h + 1) * 512)
                        dve.wait_ge(nm_hi_ready, 2 * g + h + 1)
                        lo_part(nm_lo[:, cols], fbk[(N0 + h) % 3][:], nm_hi[:, cols])\
                            .then_inc(nm_lo_ready, 1)

            steps(dve, step)

        @block.tensor
        def _(pe):
            def products(out_ap, pairs, start, stop):
                terms = [t for lh, ll, rh, rl in pairs for t in ((lh, rh), (lh, rl), (ll, rh))]
                for n, (lhs, rhs) in enumerate(terms):
                    last = pe.matmul(out_ap, lhs, rhs, start=start and n == 0,
                                     stop=stop and n == len(terms) - 1)
                return last

            w_tap = raw2.rearrange("p (i k) -> p k i", k=TAPS)
            gate_order = (2, 0, 1)

            def turn(bank, sources, at=0):
                for n, src in enumerate(sources):
                    k = src.shape[0]
                    last = pe.transpose(bank[:, at + n * P:at + n * P + k], src, ident[0:k, 0:k])
                last.then_inc(w_turned, 1)

            def turn_small():
                pe.wait_ge(ident_ready, 1)
                pe.wait_ge(raw_scaled, 1)
                pe.wait_ge(w_in, 16 * 4)
                turn(gbk[0], [raw_c1, raw_msg, raw_se])

            def turn_taps():
                pe.wait_ge(raw_scaled, 2)
                pe.wait_ge(ms_ready, 2)
                turn(gbk[0], [w_tap[:, TAPS - 1, :]], 3 * P)
                for n, bank in enumerate((gbk[1], cb[0], cb[1], cb[2])):
                    turn(bank, [w_tap[:, 4 * n + k, :] for k in range(4)])

            def turn_gates():
                pe.wait_ge(taps_copied, 5)
                pe.wait_ge(raw_scaled, 3)
                turn(cb[GX], [raw_ih[:, n, 0:P] for n in gate_order])
                turn(cb[GN], [raw_ih[:, n, P:2 * P] for n in gate_order])
                turn(cb[GH], [raw_hh[:, n, :] for n in range(3)])

            freed = {T0: (hT_ready, 2, 1), T1: (hT_ready, 2, 2), M0: (coord_ready, 3, 1),
                     M1: (coord_ready, 3, 2), M2: (coord_ready, 3, 3), C0: (h1_ready, 4, 2),
                     C1: (h1_ready, 4, 4), SR: (rows_ready, 1, 1), N0: (nm_lo_ready, 2, 1),
                     N1: (nm_lo_ready, 2, 2)}
            for b in range(GB):
                freed[J[b]] = (edge_ready, GB, b + 1)
                freed[D[b]] = (exp_ready, GB, b + 1)

            def front_bank(use, g):
                before = use - 3
                s, per, n = freed[before % FRONT]
                wait(pe, s, per * (g - (before < 0)) + n)
                return fbk[use % 3]

            def conv(par, gb, kind, section, leaves, release, released):
                wait(pe, release, released)
                for n, leaf in enumerate(leaves):
                    at, taps = leaf_at[section, leaf]
                    pairs = []
                    for k in range(taps):
                        hi, lo = (v[:, LEAF_SLOT[leaf], section * GB:(section + 1) * GB, k:k + quarter]
                                  for v in (leaf_hi, leaf_lo))
                        pairs.append((filt_hi[:, at + k, :], filt_lo[:, at + k, :], hi, lo))
                    width = GB * quarter
                    last = products(cb[kind % 3][:, n * width:(n + 1) * width], pairs, True, True)
                last.then_inc(conv_done, 1)

            def turn_nodes(par, g):
                for h in range(2):
                    bank = front_bank(T0 + h, g)
                    pe.wait_ge(hn_ready, 2 * g + h + 1)
                    for t in range(half_tiles):
                        last = pe.transpose(bank[:, t * P:(t + 1) * P], hn[par][:, h * half_tiles + t, :],
                                            ident[:])
                    last.then_inc(front_done, 1)

            def conv1(par, g):
                for h in range(2):
                    bank = front_bank(C0 + h, g)
                    pe.wait_ge(hT_split, 4 * g + 2 * h + 2)
                    cols = slice(h * 512, (h + 1) * 512)
                    products(bank[:], [(c1_hi[:], c1_lo[:], hT_hi[par][:, cols], hT_lo[par][:, cols])],
                             True, True).then_inc(front_done, 1)

            def messages(par, g):
                for n in range(3):
                    bank = front_bank(M0 + n, g)
                    pe.wait_ge(hT_ready, 2 * g + 2)
                    for t in range(3 * n, min(3 * n + 3, tiles)):
                        dst = bank[:, (t - 3 * n) * MS:(t - 3 * n + 1) * MS]
                        pe.matmul(dst, ones_bf[:], bias_parts[:, 4 * P:4 * P + MS], start=True, stop=False)
                        last = pe.matmul(dst, hT[par][:, t * P:(t + 1) * P], w_ms[:], start=False, stop=True)
                    last.then_inc(front_done, 1)

            def turn_rows(g):
                bank = front_bank(SR, g)
                pe.wait_ge(stage_ready, g + 1)
                for n in range(4):
                    last = pe.transpose(bank[:, n * P:(n + 1) * P],
                                        stage[:, n // 2, n % 2].rearrange("p b r -> p (b r)"), ident[:])
                last.then_inc(front_done, 1)

            def graph_edges(g, b):
                bank = front_bank(J[b], g)
                pe.wait_ge(adj_in[b], 16 * (g + 1))
                for mt in range(2):
                    for nt in range(2):
                        last = pe.transpose(bank[:, mt * nodes + nt * P:mt * nodes + (nt + 1) * P],
                                            adj_sb[:, b, nt, mt * P:(mt + 1) * P], ident[:])
                last.then_inc(front_done, 1)
                bank = front_bank(D[b], g)
                pe.wait_ge(rows_ready, g + 1)
                mine = slice(SLOT * b, SLOT * b + KDIST)
                for mt in range(2):
                    last = pe.matmul(bank[:, mt * nodes:(mt + 1) * nodes],
                                     rows[mine, mt * P:(mt + 1) * P], rows[mine, 2 * P:4 * P],
                                     start=True, stop=True)
                last.then_inc(front_done, 1)

            def gather(g, h):
                bank = front_bank(N0 + h, g)
                pe.wait_ge(edge_ready, GB * g + 2 * h + 2)
                pe.wait_ge(msg_ready, 3 * g + 3)
                for b in (2 * h, 2 * h + 1):
                    for mt in range(2):
                        last = pe.matmul(bank[:, (b % 2) * nodes:(b % 2 + 1) * nodes],
                                         msg[:, 2 * b + mt, :], edge[:, b, mt, :], start=mt == 0,
                                         stop=mt == 1)
                last.then_inc(front_done, 1)

            def gate_start(par, gb, t):
                wait(pe, q_ready, tiles * gb + t - 1)
                cols = slice(t * P, (t + 1) * P)
                bank = gbk[t % 2]
                pe.matmul(bank[:], ones_bf[:], bias_parts[:, 0:4 * P], start=True, stop=False)
                products(bank[:, P:4 * P], [(hT_hi[par][:, cols], hT_lo[par][:, cols],
                                             gate_hi[:, GH], gate_lo[:, GH])], False, False)
                if t == 0:
                    pe.wait_ge(nm_lo_ready, 2 * gb + 2)
                products(bank[:, 0:3 * P], [(nm_hi[:, cols], nm_lo[:, cols],
                                             gate_hi[:, GN], gate_lo[:, GN])], False, False)

            def gate_end(gb, t):
                cols = slice(t * P, (t + 1) * P)
                bank = gbk[t % 2]
                if t == 0:
                    pe.wait_ge(xc_hi_ready, gb + 1)
                    pe.wait_ge(xc_lo_ready, gb + 1)
                products(bank[:, 0:3 * P], [(xc_hi[:, cols], xc_lo[:, cols],
                                             gate_hi[:, GX], gate_lo[:, GX])], False, True)\
                    .then_inc(gate_done, 1)

            def step(it, par, front, back):
                g = 2 * it + par
                gb = g - 1
                first = isinstance(it, int) and it == 0 and par == 0
                if first:
                    turn_small()
                if isinstance(it, int) and it == 0 and par:
                    pe.wait_ge(filt_hi_ready, len(leaf_at))
                    pe.wait_ge(filt_lo_ready, len(leaf_at))
                    pe.wait_ge(gate_hi_ready, 3)
                    pe.wait_ge(gate_lo_ready, 3)
                if back:
                    pe.wait_ge(leaf_hi_ready, 2 * g)
                    pe.wait_ge(leaf_lo_ready, 2 * g)
                    conv(par, gb, CV_BB, B, (B,), y_ready, 2 * gb - 1)
                    conv(par, gb, CV_B, B, (A, C), p_copied, 3 * gb)
                    conv(par, gb, CV_AB, A, (B,), y_ready, 2 * gb)
                    conv(par, gb, CV_A, A, (A, C), p_copied, 3 * gb + 1)
                if front:
                    turn_nodes(par, g)
                if first:
                    turn_taps()
                if back:
                    conv(par, gb, CV_CB, C, (B,), mb_ready, gb + 1)
                if first:
                    pe.wait_ge(zero_ready, ZEROS)
                    pe.wait_ge(part_placed, 4)
                    pe.wait_ge(c1_ready, 2)
                if front:
                    messages(par, g)
                if back:
                    conv(par, gb, CV_C, C, (A, C), p_copied, 3 * gb + 2)
                if front:
                    conv1(par, g)
                if first:
                    turn_gates()
                if front:
                    turn_rows(g)
                if back:
                    gate_start(1 - par, gb, 0)
                if front:
                    graph_edges(g, 0)
                if back:
                    gate_start(1 - par, gb, 1)
                if front:
                    graph_edges(g, 1)
                for t in range(tiles):
                    if back:
                        if t > 1:
                            gate_start(1 - par, gb, t)
                        gate_end(gb, t)
                    if front and t in (2, 4):
                        graph_edges(g, 2 if t == 2 else 3)
                if front:
                    gather(g, 0)
                    gather(g, 1)

            steps(pe, step)


_INS = ["x", "adj"] + ["L0_gnn_" + n for n in (
    "w_se", "b_se", "conv1_w", "bn1_g", "bn1_b", "bn1_m", "bn1_v", "conv2_w", "bn2_g", "bn2_b", "bn2_m",
    "bn2_v", "w_msg", "b_msg", "w_ih", "b_ih", "w_hh", "b_hh")]


def kernel(**inputs):
    import numpy as np
    import concourse.bacc as bacc
    from concourse.bass_utils import run_bass_kernel_spmd

    nc = bacc.Bacc("TRN2", target_bir_lowering=False, num_devices=1)
    arrays, args = {}, []
    for name in _INS:
        a = np.ascontiguousarray(inputs[name])
        arrays[f"in_{name}"] = a
        args.append(nc.dram_tensor(f"in_{name}", a.shape, F32, kind="ExternalInput").ap())
    shape = arrays["in_x"].shape
    out = nc.dram_tensor("out_0", shape, F32, kind="ExternalOutput").ap()
    build(nc, *args, out)
    r = run_bass_kernel_spmd(nc, [arrays], core_ids=[0])
    return r.results[0]["out_0"]
```

```python
from contextlib import ExitStack

import concourse.bass as bass
from concourse import mybir

F32 = mybir.dt.float32
F32R = mybir.dt.float32r
ALU = mybir.AluOpType
ACT = mybir.ActivationFunctionType
AX = mybir.AxisListType

P = 128
GB = 4
EPS = 1e-5
TAPS = 17
HALO = TAPS // 2
LEAVES = 3
A, B, C = range(LEAVES)
MS = 132
SLOT = 32
ROWS = 5
KDIST = 4 * ROWS

(T0, T1, M0, M1, M2, C0, C1, SR, D0, J0, D1, J1, D2, J2, D3, J3, N0, N1) = range(18)
J = (J0, J1, J2, J3)
D = (D0, D1, D2, D3)
FRONT = 18
(CV_BB, CV_B, CV_AB, CV_A, CV_CB, CV_C) = range(6)
CONV = 6
FILTERS = [(s, leaf) for s in (B, A, C) for leaf in (B, A, C)]
LEAF_ORDER = (B, A, C)


def leaf_taps():
    even = {A: (TAPS + 1) // 2, B: (TAPS + 1) // 2, C: TAPS // 2}
    place, at = {}, 0
    for s in (A, B, C):
        for leaf in (A, B, C):
            n = even[s] // 2 if leaf == C else (even[s] + 1) // 2
            place[s, leaf] = (at, n)
            at += n
    return place, at


def build(nc, x, adj, w_se, b_se, conv1_w, bn1_g, bn1_b, bn1_m, bn1_v, conv2_w, bn2_g, bn2_b,
          bn2_m, bn2_v, w_msg, b_msg, w_ih, b_ih, w_hh, b_hh, out):
    graphs, nodes, feats = x.shape
    assert feats == P and nodes == 2 * P and graphs % (2 * GB) == 0
    groups = graphs // GB
    tiles = GB * nodes // P
    half_tiles = tiles // 2
    quarter = nodes // 4
    xw = (nodes + 2 * HALO) // 2
    lw = xw // 2
    leaf_at, n_filters = leaf_taps()
    SEC = GB * lw

    ctx = ExitStack()
    with ctx:
        def sb(name, shape, dt=F32):
            return ctx.enter_context(nc.sbuf_tensor(name, shape, dt))

        def sem(name):
            return ctx.enter_context(nc.semaphore(name))

        x_ring = sb("x_ring", [P, 4 * tiles * P])
        hn = [sb(f"hn{i}", [P, tiles, P]) for i in range(2)]
        hT = [sb(f"hT{i}", [P, tiles * P]) for i in range(2)]
        hT_hi = [sb(f"hT_hi{i}", [P, tiles * P], F32R) for i in range(2)]
        hT_lo = [sb(f"hT_lo{i}", [P, tiles * P], F32R) for i in range(2)]
        Xe = sb("Xe", [P, GB, xw])
        sect = sb("sect", [P, LEAVES, GB, xw])
        diff = sb("diff", [P, 2, LEAVES * GB, lw])
        leaf_hi = sb("leaf_hi", [P, LEAVES, LEAVES * GB, lw], F32R)
        leaf_lo = sb("leaf_lo", [P, LEAVES, LEAVES * GB, lw], F32R)
        LEAF_SLOT = {A: 0, C: 1, B: 2}
        filt_hi = sb("filt_hi", [P, n_filters, P], F32R)
        filt_lo = sb("filt_lo", [P, n_filters, P], F32R)
        c1_hi = sb("c1_hi", [P, P], F32R)
        c1_lo = sb("c1_lo", [P, P], F32R)
        w_ms = sb("w_ms", [P, MS])
        gate_hi_mem = sb("gate_hi", [P, 10 * P], F32R)
        gate_lo = sb("gate_lo", [P, 3, 3 * P], F32R)
        GX, GN, GH = range(3)
        gate_hi = [gate_hi_mem[:, at * P:(at + 3) * P] for at in (0, 3, 7)]
        gate_hi_wide = gate_hi_mem[:, 6 * P:10 * P]
        ident = sb("ident", [P, P])
        BIAS_W = 4 * P + MS
        bias = sb("bias", [P, BIAS_W])
        scratch = sb("scratch", [P, 6400])
        xc_hi = sb("xc_hi", [P, tiles * P], F32R)
        xc_lo = sb("xc_lo", [P, tiles * P], F32R)
        nm_hi = sb("nm_hi", [P, tiles * P], F32R)
        nm_lo = sb("nm_lo", [P, tiles * P], F32R)
        adj_sb = sb("adj_sb", [P, GB, 2, nodes])
        edge = sb("edge", [P, GB, 2, nodes])
        msg = sb("msg", [P, tiles, MS])
        stage = sb("stage", [P, 2, 2, GB, SLOT])
        rows = sb("rows", [P, 4 * P], F32R)
        stats = sb("stats", [P, tiles, 6])
        spread = sb("spread", [P, tiles])
        mean = sb("mean", [P, tiles])
        veps = sb("veps", [P, tiles])
        rstd = sb("rstd", [P, tiles])
        neg_half = sb("neg_half", [P, tiles])
        coord2 = sb("coord2", [P, tiles, 3])
        dist_f = sb("dist_f", [P, 2, 2, GB, ROWS])
        bn = sb("bn", [P, 2, 4])
        bn_s = sb("bn_s", [P, 4, 2])

        off = 0

        def carve(n):
            nonlocal off
            off += n
            return scratch[:, off - n:off]
        gate = carve(tiles * 4 * P).rearrange("p (t c) -> p t c", t=tiles)
        ysum = carve(tiles * P)
        pcopy = carve(3 * GB * quarter).rearrange("p (s c) -> p s c", s=3)
        m_b = carve(2 * GB * quarter)
        off = 0
        raw2 = carve(TAPS * P)
        w2T = carve(TAPS * P).rearrange("p (k o) -> p k o", k=TAPS)
        fb = carve((TAPS + 1) // 2 * P).rearrange("p (k o) -> p k o", o=P)
        fsum = raw2[:, 0:14 * P].rearrange("p (k o) -> p k o", o=P)
        edge_flat = edge[:].rearrange("p b t n -> p (b t n)")
        raw_ih = edge_flat[:, 0:6 * P].rearrange("p (g c) -> p g c", g=3)
        raw_hh = edge_flat[:, 6 * P:9 * P].rearrange("p (g c) -> p g c", g=3)
        raw_c1 = edge_flat[:, 9 * P:10 * P]
        raw_msg = edge_flat[:, 10 * P:11 * P]
        raw_se = edge_flat[0:3, 11 * P:12 * P]
        raw_bhh = edge_flat[:, 12 * P:15 * P]

        cb = [ctx.enter_context(nc.psum_tensor(f"conv_bank{i}", [P, 512], F32)) for i in range(3)]
        gbk = [ctx.enter_context(nc.psum_tensor(f"gate_bank{i}", [P, 512], F32)) for i in range(2)]
        fbk = [ctx.enter_context(nc.psum_tensor(f"front_bank{i}", [P, 512], F32)) for i in range(3)]

        gate_bank = [(gbk + cb)[t % 5] for t in range(tiles)]
        gate_raw_bank = {GX: gbk[0], GN: gbk[1], GH: cb[CV_AB % 3]}

        x_in = [sem(f"x_in{i}") for i in range(2)]
        adj_in = [sem(f"adj_in{b}") for b in range(GB)]
        out_stored = [sem(f"out_stored{h}") for h in range(2)]
        front_done = sem("front_done")
        conv_done = sem("conv_done")
        gate_done = sem("gate_done")
        hT_ready = sem("hT_ready")
        h1_ready = sem("h1_ready")
        p_copied = sem("p_copied")
        msg_ready = sem("msg_ready")
        rows_ready = sem("rows_ready")
        exp_ready = sem("exp_ready")
        xc_hi_ready = sem("xc_hi_ready")
        leaf_hi_ready = sem("leaf_hi_ready")
        rz_ready = sem("rz_ready")
        n_ready = sem("n_ready")
        nm_hi_ready = sem("nm_hi_ready")
        ln_link = sem("ln_link")
        veps_ready = sem("veps_ready")
        hn_ready = sem("hn_ready")
        hT_split = sem("hT_split")
        mb_ready = sem("mb_ready")
        y_ready = sem("y_ready")
        msg_biased = sem("msg_biased")
        gate_biased = sem("gate_biased")
        row_link = sem("row_link")
        stage_ready = sem("stage_ready")
        edge_ready = sem("edge_ready")
        xc_lo_ready = sem("xc_lo_ready")
        leaf_lo_ready = sem("leaf_lo_ready")
        m_ready = sem("m_ready")
        q_ready = sem("q_ready")
        d_ready = sem("d_ready")
        out_ready = sem("out_ready")
        nm_lo_ready = sem("nm_lo_ready")
        rstd_ready = sem("rstd_ready")
        res_added = sem("res_added")
        diff_ready = sem("diff_ready")
        p_ready = sem("p_ready")
        ident_ready = sem("ident_ready")
        pool_link = sem("pool_link")
        zero_ready = sem("zero_ready")
        bn_in = sem("bn_in")
        small_in = sem("small_in")
        w_in = sem("w_in")
        bias_in = sem("bias_in")
        w2_in = sem("w2_in")
        bn_veps = sem("bn_veps")
        bn_powed = sem("bn_powed")
        bn_ready = sem("bn_ready")
        raw_scaled = sem("raw_scaled")
        w_turned = sem("w_turned")
        c1_ready = sem("c1_ready")
        ms_ready = sem("ms_ready")
        taps_copied = sem("taps_copied")
        tap_sums = sem("tap_sums")
        own_tap_sums = sem("own_tap_sums")
        filt_hi_ready = sem("filt_hi_ready")
        filt_lo_ready = sem("filt_lo_ready")
        gate_hi_ready = sem("gate_hi_ready")
        gate_lo_ready = sem("gate_lo_ready")
        bias_set = sem("bias_set")

        block = ctx.enter_context(nc.Block())

        def wait(eng, s, value):
            if not isinstance(value, int) or value > 0:
                eng.wait_ge(s, value)

        def steps(eng, step):
            step(0, 0, True, False)
            step(0, 1, True, True)
            with eng.Fori(1, groups // 2) as it:
                for par in range(2):
                    step(it, par, True, True)
            step(groups // 2, 0, False, True)

        def slot(it, par):
            return ((it % 2) * 2 + par) * (tiles * P)

        def slot_before(it, par):
            return slot(it, 0) if par else (((it + 1) % 2) * 2 + 1) * (tiles * P)

        def slot_two_before(it, par):
            return slot(it + 1, par)

        ZEROS = 11
        LINKS, NORM_LINKS = 7, 7
        W_SMALL, W_TAPS = 1, 6
        SUM_AT = {A: 0, B: 5, C: 10}
        EXP_AT, EDGE_AT = {1: 2, 3: 3}, {0: 1, 2: 2, 4: 3}

        def phases(ap, l1):
            return ap.rearrange("p (b i l m) -> p l b i m", b=GB, i=quarter, l=2)[:, :, :, :, l1]

        def by_phase(ap):
            return ap.rearrange("p (l b i) -> p l b i", l=2, b=GB)

        def for_both(ap):
            return ap.rearrange("p (l b i) -> p l b i", l=1, b=GB).broadcast_to([P, 2, GB, quarter])

        def half_of_x(at, h):
            at = at + h * half_tiles * P
            return x_ring[:, bass.ds(at, half_tiles * P)].rearrange("p (t c) -> p t c", c=P)

        def ms_bank(n, nt):
            return fbk[(M0 + n) % 3][:, 0:nt * MS].rearrange("p (t c) -> p t c", c=MS)

        samples = sect[:].rearrange("p s b n -> p (s b) n")
        odd_samples = samples[:, :, 1:xw:2]

        def leaf_parts(leaf, hi_lo):
            src = {A: diff[:, 0], B: odd_samples, C: diff[:, 1]}[leaf]
            return src, hi_lo[:, LEAF_SLOT[leaf]]

        def tap_bank(n):
            if n == 4:
                return w2T[:, TAPS - 1, :], gbk[0][:, 3 * P:4 * P]
            dst = w2T[:, 4 * n:4 * n + 4, :].rearrange("p k o -> p (k o)")
            return dst, (gbk[1], cb[0], cb[1], cb[2])[n][:]

        def sum_section(eng, s):
            n_even, n_odd = leaf_at[s, A][1], leaf_at[s, C][1]
            if n_even > n_odd:
                eng.tensor_copy(fsum[:, SUM_AT[s] + n_odd, :], half_run(s, 0, n_even)[:, n_odd, :])
            eng.tensor_tensor(fsum[:, SUM_AT[s]:SUM_AT[s] + n_odd, :], half_run(s, 0, n_odd),
                              half_run(s, 1, n_odd), ALU.add)\
               .then_inc(tap_sums if s == B else own_tap_sums, 1)

        def half_run(s, first, n):
            if s == B:
                return fb[:, first:first + 2 * n - 1:2, :]
            k = 2 * first + (s == C)
            return w2T[:, k:k + 4 * n - 3:4, :]

        def leaf_source(s, leaf):
            n = leaf_at[s, leaf][1]
            if leaf == A:
                return half_run(s, 0, n)
            if leaf == C:
                return half_run(s, 1, n)
            return fsum[:, SUM_AT[s]:SUM_AT[s] + n, :]

        @block.sync
        def _(sp):
            def load_x(it, par, g):
                at = slot(it, par)
                sp.dma_start(x_ring[:, bass.ds(at, tiles * P)].rearrange("p (b t c) -> p b t c", b=GB, t=2),
                             x_groups[g]).then_inc(x_in[par], 16)

            x_groups = x.rearrange("(g b) (t p) c -> g p b t c", b=GB, p=P)
            o_groups = out.rearrange("(g b) (t p) c -> g p b t c", b=GB, p=P)
            a_graphs = adj.rearrange("(g b) (t p) m -> g b p t m", b=GB, p=P)

            def step(it, par, front, back, load):
                g = 2 * it + par
                first = isinstance(it, int) and g == 0
                at = slot_before(it, par)
                if front:
                    for b in range(GB):
                        wait(sp, front_done, FRONT * (g - 1) + J[b] + 1)
                        sp.dma_start(adj_sb[:, b, :, :], a_graphs[g, b]).then_inc(adj_in[b], 16)
                if back:
                    for h in range(2):
                        wait(sp, out_stored[h], 16 * (g - 1))
                if first:
                    load_x(0, 1, 1)
                if load:
                    sp.wait_ge(hn_ready, 2 * g + 2)
                    load_x(it + 1, par, g + 2)
                if back:
                    for h in range(2):
                        sp.wait_ge(out_ready, 2 * (g - 1) + h + 1)
                        half = GB // 2
                        sp.dma_start(
                            o_groups[g - 1][:, half * h:half * h + half],
                            x_ring[:, bass.ds(at + h * half_tiles * P, half_tiles * P)]
                            .rearrange("p (b t c) -> p b t c", b=half, t=2),
                        ).then_inc(out_stored[h], 16)

            load_x(0, 0, 0)
            sp.dma_start(raw2, conv2_w.rearrange("o i k -> o (i k)")).then_inc(w2_in, 16)
            sp.dma_start(raw_msg, w_msg).then_inc(small_in, 16)
            sp.dma_start(raw_se, w_se).then_inc(small_in, 16)
            for dst, src in ((bias[:, 4 * P:5 * P], b_msg), (bias[:, 5 * P:5 * P + 3], b_se),
                             (bias[:, 0:P], b_ih[2 * P:3 * P]), (bias[:, P:3 * P], b_ih[0:2 * P]),
                             (raw_bhh, b_hh)):
                row = src.rearrange("(a n) -> a n", a=1)
                sp.dma_start(dst, row.broadcast_to([P, row.shape[1]])).then_inc(bias_in, 16)
            sp.dma_start(raw_hh, w_hh.rearrange("(g o) c -> o g c", g=3)).then_inc(w_in, 16)
            sp.dma_start(raw_ih, w_ih.rearrange("(g o) c -> o g c", g=3)).then_inc(w_in, 16)
            step(0, 0, True, False, True)
            step(0, 1, True, True, True)
            with sp.Fori(1, groups // 2 - 1) as it:
                for par in range(2):
                    step(it, par, True, True, True)
            step(groups // 2 - 1, 0, True, True, False)
            step(groups // 2 - 1, 1, True, True, False)
            step(groups // 2, 0, False, True, False)
            for h in range(2):
                sp.wait_ge(out_stored[h], 16 * groups)

        @block.gpsimd
        def _(pool):
            pool.memset(ident[:], 0.0).then_inc(pool_link, 1)
            pool.wait_ge(pool_link, 1)
            pool.affine_select(out=ident[:], in_=ident[:], compare_op=ALU.not_equal, fill=1.0, base=0,
                               pattern=[[-1, P]], channel_multiplier=1).then_inc(ident_ready, 1)
            pad, end = HALO // 2, HALO // 2 + nodes // 2
            pool.memset(neg_half[:], -0.5).then_inc(zero_ready, 1)
            for v in (Xe[:], sect[:, B]):
                pool.memset(v[:, :, 0:pad], 0.0).then_inc(zero_ready, 1)
                pool.memset(v[:, :, end:xw], 0.0).then_inc(zero_ready, 1)
            pool.memset(sect[:, C, :, xw - 1:xw], 0.0).then_inc(zero_ready, 1)
            pool.memset(diff[:, 1, :, lw - 1:lw], 0.0).then_inc(zero_ready, 1)
            pool.memset(stage[:], 0.0).then_inc(zero_ready, 1)
            pool.memset(dist_f[:, 0, :, :, 3:4], -1.0).then_inc(zero_ready, 1)
            pool.memset(dist_f[:, 1, :, :, 4:5], 1.0).then_inc(zero_ready, 1)
            pool.memset(gate_hi_mem[:, 6 * P:7 * P].bitcast(F32), 0.0).then_inc(zero_ready, 1)
            pool.wait_ge(zero_ready, ZEROS)

            def step(it, par, front, back):
                g = 2 * it + par
                gb = g - 1
                if front:
                    pool.wait_ge(veps_ready, g + 1)
                    wait(pool, hn_ready, 2 * g)
                    pool.tensor_tensor(rstd[:], veps[:], neg_half[:], ALU.pow).then_inc(rstd_ready, 1)
                if isinstance(it, int) and g == 0:
                    pool.wait_ge(bn_veps, 1)
                    pool.tensor_tensor(bn_s[:, 1], bn_s[:, 0], neg_half[:, 0:2],
                                       ALU.pow).then_inc(bn_powed, 1)
                if back:
                    pool.wait_ge(mb_ready, gb + 1)
                    wait(pool, xc_hi_ready, 2 * gb)
                    wait(pool, xc_lo_ready, 2 * gb)
                    for l1 in range(2):
                        pool.tensor_tensor(phases(ysum, l1), phases(hT[1 - par][:], l1), by_phase(m_b),
                                           ALU.add).then_inc(res_added, 1)
                    pool.wait_ge(p_copied, 3 * gb + 2)
                    pool.wait_ge(res_added, 4 * gb + 1)
                    pool.tensor_tensor(phases(ysum, 0), phases(ysum, 0), for_both(pcopy[:, 1, :]),
                                       ALU.add).then_inc(res_added, 1)
                    pool.wait_ge(p_copied, 3 * gb + 3)
                    pool.wait_ge(res_added, 4 * gb + 2)
                    pool.tensor_tensor(phases(ysum, 1), phases(ysum, 1), for_both(pcopy[:, 2, :]),
                                       ALU.add).then_inc(res_added, 1)
                if front:
                    pool.wait_ge(h1_ready, 4 * g + 4)
                    pool.tensor_tensor(sect[:, A], Xe[:], sect[:, B], ALU.subtract).then_inc(diff_ready, 1)
                    pool.tensor_tensor(sect[:, C, :, 0:xw - 1], Xe[:, :, 1:xw], sect[:, B, :, 0:xw - 1],
                                       ALU.subtract).then_inc(diff_ready, 1)
                if front:
                    pool.wait_ge(diff_ready, 4 * g + 2)
                    wait(pool, leaf_hi_ready, LEAVES * g)
                    wait(pool, leaf_lo_ready, LEAVES * g)
                    pool.tensor_tensor(diff[:, 0], samples[:, :, 0:xw:2], samples[:, :, 1:xw:2],
                                       ALU.subtract).then_inc(diff_ready, 1)
                    pool.tensor_tensor(diff[:, 1, :, 0:lw - 1], samples[:, :, 2:xw:2],
                                       samples[:, :, 1:xw - 2:2], ALU.subtract).then_inc(diff_ready, 1)
                if isinstance(it, int) and g == 0:
                    pool.wait_ge(taps_copied, 5)
                    sum_section(pool, A)
                    sum_section(pool, C)
                if back:
                    for h in range(2):
                        pool.wait_ge(n_ready, 2 * gb + h + 1)
                        part = half_of_x(slot_before(it, par), h)
                        ts = slice(h * half_tiles, (h + 1) * half_tiles)
                        pool.tensor_tensor(part, part, gate[:, ts, 0:P], ALU.add).then_inc(p_ready, 1)

            steps(pool, step)

        @block.scalar
        def _(act):
            def column(vec):
                return vec.rearrange("(p a) -> p a", a=1)

            act.dma_start(raw_c1, conv1_w.rearrange("o i k -> o (i k)")).then_inc(bn_in, 16)
            for n, vecs in enumerate(((bn1_v, bn1_g, bn1_b, bn1_m), (bn2_v, bn2_g, bn2_b, bn2_m))):
                for k, vec in enumerate(vecs):
                    act.dma_start(bn[:, n, k:k + 1], column(vec)).then_inc(bn_in, 16)

            def conv1_hi():
                act.wait_ge(w_turned, W_SMALL)
                act.activation(c1_hi[:], gbk[0][:, 0:P], ACT.Copy).then_inc(c1_ready, 1)

            def taps(n):
                act.wait_ge(w_turned, W_SMALL + n + 1)
                dst, src = tap_bank(n)
                act.activation(dst, src, ACT.Copy).then_inc(taps_copied, 1)

            def filters_hi(section):
                act.wait_ge(*{B: (tap_sums, 3), A: (own_tap_sums, 1), C: (own_tap_sums, 2)}[section])
                for key in FILTERS:
                    if key[0] == section:
                        at, k = leaf_at[key]
                        act.activation(filt_hi[:, at:at + k, :], leaf_source(*key), ACT.Copy)\
                           .then_inc(filt_hi_ready, 1)

            def gates_hi(n):
                act.wait_ge(w_turned, W_TAPS + n + 1)
                act.activation(gate_hi[n], gate_raw_bank[n][:, 0:3 * P], ACT.Copy).then_inc(gate_hi_ready, 1)

            def edges(g, b):
                act.wait_ge(front_done, FRONT * g + D[b] + 1)
                act.activation(edge[:, b].rearrange("p t n -> p (t n)"), fbk[D[b] % 3][:],
                               ACT.Exp).then_inc(exp_ready, 1)

            def shared(gb, n, kind):
                act.wait_ge(conv_done, CONV * gb + kind + 1)
                if n == 0:
                    wait(act, mb_ready, gb)
                    act.activation(pcopy[:, 0, :], cb[kind % 3][:, 0:GB * quarter], ACT.Identity,
                                   bias=bn_s[:, 3, 1:2]).then_inc(p_copied, 1)
                else:
                    wait(act, res_added, 4 * gb)
                    act.activation(pcopy[:, n, :], cb[kind % 3][:, 0:GB * quarter],
                                   ACT.Copy).then_inc(p_copied, 1)

            def relu_conv(gb, h):
                wait(act, gate_done, tiles * gb)
                act.wait_ge(y_ready, 2 * gb + 2)
                cols = slice(h * 512, (h + 1) * 512)
                act.activation(xc_hi[:, cols], ysum[:, cols], ACT.Relu).then_inc(xc_hi_ready, 1)

            def leaves_hi(g, leaf):
                wait(act, conv_done, CONV * g)
                act.wait_ge(*((h1_ready, 4 * g + 4) if leaf == B else (diff_ready, 4 * g + 4)))
                if leaf == B:
                    act.wait_ge(diff_ready, 4 * g + 2)
                src, dst = leaf_parts(leaf, leaf_hi)
                act.activation(dst, src, ACT.Copy).then_inc(leaf_hi_ready, 1)

            def gathered_hi(g):
                wait(act, gate_done, tiles * g)
                for h in range(2):
                    act.wait_ge(front_done, FRONT * g + N0 + h + 1)
                    act.activation(nm_hi[:, h * 512:(h + 1) * 512], fbk[(N0 + h) % 3][:],
                                   ACT.Copy).then_inc(nm_hi_ready, 1)

            def step(it, par, front, back):
                g = 2 * it + par
                gb = g - 1
                first = isinstance(it, int) and g == 0
                second = isinstance(it, int) and g == 1
                if back:
                    shared(gb, 0, CV_BB)
                if second:
                    for n in range(3):
                        gates_hi(n)
                    gathered_hi(0)
                if back:
                    shared(gb, 1, CV_AB)
                if front:
                    wait(act, front_done, FRONT * (g - 2) + M2 + 1)
                    wait(act, hT_split, 4 * (g - 1))
                    wait(act, res_added, 4 * (g - 1))
                    for h in range(2):
                        act.wait_ge(front_done, FRONT * g + T0 + h + 1)
                        act.activation(hT[par][:, h * 512:(h + 1) * 512], fbk[(T0 + h) % 3][:],
                                       ACT.Relu).then_inc(hT_ready, 1)
                if back:
                    shared(gb, 2, CV_CB)
                if first:
                    conv1_hi()
                    taps(0)
                if front:
                    for n in range(3):
                        act.wait_ge(msg_biased, 3 * g + n + 1)
                        v = msg[:, 3 * n:min(3 * n + 3, tiles), 0:P]
                        act.activation(v, v, ACT.Relu).then_inc(msg_ready, 1)
                    if first:
                        taps(1)
                    wait(act, diff_ready, 4 * g)
                    wait(act, leaf_lo_ready, LEAVES * g)
                    wait(act, leaf_hi_ready, LEAVES * g)
                    if first:
                        act.wait_ge(bn_ready, 3)
                        act.wait_ge(zero_ready, ZEROS)
                    for h in range(2):
                        act.wait_ge(front_done, FRONT * g + C0 + h + 1)
                        v = fbk[(C0 + h) % 3][:].rearrange("p (b n m) -> p b n m", b=2, m=2)
                        pad = HALO // 2
                        for m, dst in ((0, Xe[:, 2 * h:2 * h + 2]), (1, sect[:, B, 2 * h:2 * h + 2])):
                            act.activation(dst[:, :, pad:pad + nodes // 2], v[:, :, :, m], ACT.Relu,
                                           bias=bn_s[:, 3, 0:1]).then_inc(h1_ready, 1)
                        if back and h == 0:
                            relu_conv(gb, 0)
                    if first:
                        taps(4)
                    act.wait_ge(front_done, FRONT * g + SR + 1)
                    act.activation(rows[:], fbk[SR % 3][:], ACT.Copy).then_inc(rows_ready, 1)
                    edges(g, 0)
                    if first:
                        edges(0, 1)
                        filters_hi(B)
                        edges(0, 2)
                        leaves_hi(0, B)
                        edges(0, 3)
                        leaves_hi(0, A)
                        leaves_hi(0, C)
                        filters_hi(A)
                        filters_hi(C)
                        return
                elif back:
                    relu_conv(gb, 0)
                if back:
                    relu_conv(gb, 1)
                if front:
                    edges(g, 1)
                for t in range(tiles):
                    if back:
                        act.wait_ge(gate_biased, tiles * gb + t + 1)
                        rz = gate[:, t, P:3 * P]
                        act.activation(rz, rz, ACT.Tanh, scale=0.5).then_inc(rz_ready, 1)
                    if front and t in EXP_AT:
                        edges(g, EXP_AT[t])
                    if front and t in (2, 3, 4):
                        leaves_hi(g, LEAF_ORDER[t - 2])
                    if back and t == 5:
                        new_state(gb, 0)
                if back:
                    new_state(gb, 1)
                if front:
                    gathered_hi(g)

            def new_state(gb, h):
                act.wait_ge(q_ready, tiles // 2 * gb + half_tiles // 2 * (h + 1))
                v = gate[:, h * half_tiles:(h + 1) * half_tiles, 0:P]
                act.activation(v, v, ACT.Tanh).then_inc(n_ready, 1)

            steps(act, step)

        @block.vector
        def _(dve):
            def lo_part(out_ap, src, hi):
                return dve.tensor_tensor(out_ap, src, hi.bitcast(F32), ALU.subtract)

            def batch_norms():
                dve.wait_ge(bn_in, 16 * 9)
                dve.tensor_scalar(bn_s[:, 0], bn[:, :, 0], EPS, None, ALU.add).then_inc(bn_veps, 1)
                set_biases()
                dve.wait_ge(bn_powed, 1)
                dve.tensor_tensor(bn_s[:, 2], bn[:, :, 1], bn_s[:, 1], ALU.mult).then_inc(bn_ready, 1)
                dve.wait_ge(bn_ready, 1)
                dve.tensor_scalar(raw_c1, raw_c1, bn_s[:, 2, 0:1], None, ALU.mult).then_inc(raw_scaled, 1)
                dve.tensor_tensor(bn_s[:, 3], bn[:, :, 3], bn_s[:, 2], ALU.mult).then_inc(bn_ready, 1)
                dve.wait_ge(bn_ready, 2)
                dve.tensor_tensor(bn_s[:, 3], bn[:, :, 2], bn_s[:, 3], ALU.subtract).then_inc(bn_ready, 1)

            def scale_conv2():
                dve.wait_ge(w2_in, 16)
                dve.tensor_scalar(raw2, raw2, bn_s[:, 2, 1:2], None, ALU.mult).then_inc(raw_scaled, 1)

            def small_weights():
                dve.wait_ge(c1_ready, 1)
                lo_part(c1_lo[:], gbk[0][:, 0:P], c1_hi[:]).then_inc(c1_ready, 1)
                dve.memset(w_ms[:, MS - 1:MS], 0.0).then_inc(ms_ready, 1)
                dve.tensor_copy(w_ms[:, 0:MS - 1], gbk[0][:, P:P + MS - 1]).then_inc(ms_ready, 1)

            def set_biases():
                dve.wait_ge(bias_in, 16 * 5)
                dve.memset(bias[:, BIAS_W - 1:BIAS_W], 0.0).then_inc(bias_set, 1)
                dve.tensor_tensor(bias[:, P:3 * P], bias[:, P:3 * P], raw_bhh[:, 0:2 * P],
                                  ALU.add).then_inc(bias_set, 1)
                dve.tensor_scalar(bias[:, 3 * P:4 * P], raw_bhh[:, 2 * P:3 * P], 0.5, None,
                                  ALU.mult).then_inc(bias_set, 1)

            def halve_state():
                dve.wait_ge(w_in, 16 * 2)
                dve.tensor_scalar(raw_hh[:, 2, :], raw_hh[:, 2, :], 0.5, None,
                                  ALU.mult).then_inc(raw_scaled, 1)

            def copy_taps():
                for n in (2, 3):
                    dve.wait_ge(w_turned, W_SMALL + n + 1)
                    dst, src = tap_bank(n)
                    dve.tensor_copy(dst, src).then_inc(taps_copied, 1)

            def sum_taps():
                dve.wait_ge(taps_copied, 5)
                dve.tensor_tensor(fb[:, 0:TAPS // 2, :], w2T[:, 0:TAPS - 1:2, :], w2T[:, 1:TAPS:2, :],
                                  ALU.add).then_inc(tap_sums, 1)
                dve.tensor_copy(fb[:, TAPS // 2, :], w2T[:, TAPS - 1, :]).then_inc(tap_sums, 1)
                dve.wait_ge(tap_sums, 2)
                sum_section(dve, B)

            def filters_lo(section):
                dve.wait_ge(*{B: (tap_sums, 3), A: (own_tap_sums, 1), C: (own_tap_sums, 2)}[section])
                for n, key in enumerate(FILTERS):
                    if key[0] == section:
                        at, k = leaf_at[key]
                        dve.wait_ge(filt_hi_ready, n + 1)
                        lo_part(filt_lo[:, at:at + k, :], leaf_source(*key),
                                filt_hi[:, at:at + k, :]).then_inc(filt_lo_ready, 1)

            def gates_lo(n):
                dve.wait_ge(gate_hi_ready, n + 1)
                lo_part(gate_lo[:, n], gate_raw_bank[n][:, 0:3 * P], gate_hi[n]).then_inc(gate_lo_ready, 1)

            def norm_stats(it, par, g):
                dve.wait_ge(x_in[par], 16 * (it + 1))
                at = slot(it, par)
                for t in range(tiles):
                    last = dve.bn_stats(stats[:, t, :], x_ring[:, bass.ds(at + t * P, P)])
                last.then_inc(ln_link, 1)
                mean_e, m2_e, mean_o, m2_o = (stats[:, :, k] for k in (1, 2, 4, 5))
                dve.wait_ge(ln_link, NORM_LINKS * g + 1)
                dve.tensor_tensor(spread[:], mean_e, mean_o, ALU.subtract).then_inc(ln_link, 1)
                dve.tensor_tensor(mean[:], mean_e, mean_o, ALU.add).then_inc(ln_link, 1)
                dve.tensor_tensor(veps[:], m2_e, m2_o, ALU.add).then_inc(ln_link, 1)
                dve.wait_ge(ln_link, NORM_LINKS * g + 4)
                dve.tensor_tensor(spread[:], spread[:], spread[:], ALU.mult).then_inc(ln_link, 1)
                dve.tensor_scalar(mean[:], mean[:], 0.5, None, ALU.mult).then_inc(ln_link, 1)
                dve.tensor_scalar(veps[:], veps[:], 1.0 / P, EPS, ALU.mult, ALU.add).then_inc(ln_link, 1)
                dve.wait_ge(ln_link, NORM_LINKS * g + 7)
                dve.scalar_tensor_tensor(veps[:], spread[:], 0.25, veps[:], ALU.mult,
                                         ALU.add).then_inc(veps_ready, 1)

            def normalise(it, par, g):
                dve.wait_ge(rstd_ready, g + 1)
                wait(dve, front_done, FRONT * (g - 2) + T1 + 1)
                at = slot(it, par)
                for t in range(tiles):
                    last = dve.tensor_scalar(hn[par][:, t, :], x_ring[:, bass.ds(at + t * P, P)],
                                             mean[:, t:t + 1], rstd[:, t:t + 1], ALU.subtract, ALU.mult)
                    if t % half_tiles == half_tiles - 1:
                        last.then_inc(hn_ready, 1)

            def split_nodes(par, g, h):
                wait(dve, gate_done, tiles * (g - 1))
                cols = slice(h * 512, (h + 1) * 512)
                dve.wait_ge(hT_ready, 2 * g + h + 1)
                dve.tensor_copy(hT_hi[par][:, cols], hT[par][:, cols]).then_inc(hT_split, 1)
                dve.wait_ge(hT_split, 4 * g + 2 * h + 1)
                lo_part(hT_lo[par][:, cols], hT[par][:, cols], hT_hi[par][:, cols]).then_inc(hT_split, 1)

            def section_b(gb):
                dve.wait_ge(conv_done, CONV * gb + CV_B + 1)
                dve.wait_ge(p_copied, 3 * gb + 1)
                wait(dve, res_added, 4 * gb)
                dve.tensor_tensor(m_b.rearrange("p (l c) -> p l c", l=2),
                                  cb[CV_B % 3][:].rearrange("p (l c) -> p l c", l=2),
                                  pcopy[:, 0:1, :].broadcast_to([P, 2, GB * quarter]),
                                  ALU.add).then_inc(mb_ready, 1)

            def outputs(gb, l1):
                kind = (CV_A, CV_C)[l1]
                dve.wait_ge(conv_done, CONV * gb + kind + 1)
                dve.wait_ge(res_added, 4 * gb + 3 + l1)
                dve.tensor_tensor(phases(ysum, l1), by_phase(cb[kind % 3][:]), phases(ysum, l1),
                                  ALU.add).then_inc(y_ready, 1)

            def bias_messages(g):
                wait(dve, front_done, FRONT * g)
                for n in range(3):
                    nt = min(3, tiles - 3 * n)
                    dve.wait_ge(front_done, FRONT * g + M0 + n + 1)
                    row = bias[:, 4 * P:].rearrange("p (t c) -> p t c", t=1)
                    dve.tensor_tensor(msg[:, 3 * n:3 * n + nt, :], ms_bank(n, nt),
                                      row.broadcast_to([P, nt, MS]), ALU.add).then_inc(msg_biased, 1)
                dve.wait_ge(msg_biased, 3 * g + 3)

            def distance_rows(g):
                turned = msg[:, :, P:P + 3].rearrange("p (b t) c -> p t b c", t=2)
                links = LINKS * g
                dve.tensor_tensor(coord2[:], msg[:, :, P:P + 3], msg[:, :, P:P + 3], ALU.mult).then_inc(row_link, 1)
                dve.tensor_scalar(dist_f[:, 0, :, :, 0:3], turned, 2.0, None, ALU.mult).then_inc(row_link, 1)
                dve.tensor_copy(dist_f[:, 1, :, :, 0:3], turned).then_inc(row_link, 1)
                dve.wait_ge(row_link, links + 3)
                dve.reduce_sum(dist_f[:, 1, :, :, 3], coord2[:].rearrange("p (b t) c -> p t b c", t=2),
                               axis=AX.X).then_inc(row_link, 1)
                dve.wait_ge(row_link, links + 4)
                dve.tensor_scalar(dist_f[:, 0, :, :, 4], dist_f[:, 1, :, :, 3], -1.0, None,
                                  ALU.mult).then_inc(row_link, 1)
                dve.wait_ge(row_link, links + 5)
                wait(dve, front_done, FRONT * (g - 1) + SR + 1)
                f = dist_f[:].rearrange("p s t b r -> p (s t b) r")
                st = stage[:].rearrange("p s t b r -> p (s t b) r")
                dve.tensor_copy(st[:, :, 0:ROWS].bitcast(F32R), f).then_inc(row_link, 1)
                dve.wait_ge(row_link, links + 6)
                dve.tensor_tensor(st[:, :, 3 * ROWS:4 * ROWS], f, st[:, :, 0:ROWS],
                                  ALU.subtract).then_inc(row_link, 1)
                dve.wait_ge(row_link, links + 7)
                half = 2 * GB
                for side, dst, src in ((0, 1, 0), (0, 2, 3), (1, 2, 0), (1, 1, 3)):
                    v = st[:, side * half:(side + 1) * half, :]
                    last = dve.tensor_copy(v[:, :, dst * ROWS:(dst + 1) * ROWS],
                                           v[:, :, src * ROWS:(src + 1) * ROWS])
                last.then_inc(stage_ready, 1)

            def edge_weights(g, b):
                dve.wait_ge(exp_ready, GB * g + b + 1)
                dve.wait_ge(front_done, FRONT * g + J[b] + 1)
                v = edge[:, b].rearrange("p t n -> p (t n)")
                dve.tensor_tensor(v, fbk[J[b] % 3][:], v, ALU.mult).then_inc(edge_ready, 1)

            def leaves_lo(g, n):
                wait(dve, conv_done, CONV * g)
                dve.wait_ge(leaf_hi_ready, LEAVES * g + n + 1)
                src, dst = leaf_parts(LEAF_ORDER[n], leaf_lo)
                hi = leaf_parts(LEAF_ORDER[n], leaf_hi)[1]
                lo_part(dst, src, hi).then_inc(leaf_lo_ready, 1)

            def relu_conv_lo(gb, h):
                wait(dve, gate_done, tiles * gb)
                dve.wait_ge(xc_hi_ready, 2 * gb + h + 1)
                cols = slice(h * 512, (h + 1) * 512)
                dve.scalar_tensor_tensor(xc_lo[:, cols], ysum[:, cols], 0.0, xc_hi[:, cols].bitcast(F32),
                                         ALU.max, ALU.subtract).then_inc(xc_lo_ready, 1)

            def gathered_lo(g):
                for h in range(2):
                    cols = slice(h * 512, (h + 1) * 512)
                    dve.wait_ge(nm_hi_ready, 2 * g + h + 1)
                    lo_part(nm_lo[:, cols], fbk[(N0 + h) % 3][:], nm_hi[:, cols])\
                        .then_inc(nm_lo_ready, 1)

            def bias_gates(gb, t):
                dve.wait_ge(gate_done, tiles * gb + t + 1)
                if t == 0:
                    wait(dve, p_ready, 2 * gb)
                    wait(dve, d_ready, 4 * gb)
                dve.tensor_tensor(gate[:, t, :], gate_bank[t][:], bias[:, 0:4 * P],
                                  ALU.add).then_inc(gate_biased, 1)

            def new_gates(gb, pair):
                n = tiles // 2 * gb + pair + 1
                dve.wait_ge(rz_ready, tiles * gb + 2 * pair + 2)
                gi, r, gh = (gate[:, 2 * pair:2 * pair + 2, k * P:(k + 1) * P] for k in (0, 1, 3))
                dve.scalar_tensor_tensor(gh, r, 1.0, gh, ALU.add, ALU.mult).then_inc(m_ready, 1)
                dve.wait_ge(m_ready, n)
                dve.tensor_tensor(gi, gi, gh, ALU.add).then_inc(q_ready, 1)

            def finish(at, nodes_before, gb, h):
                ts = slice(h * half_tiles, (h + 1) * half_tiles)
                dve.wait_ge(n_ready, 2 * gb + h + 1)
                n, z, d = (gate[:, ts, k * P:(k + 1) * P] for k in (0, 2, 3))
                dve.scalar_tensor_tensor(d, nodes_before[:, ts, :], 0.0, n, ALU.max,
                                         ALU.subtract).then_inc(d_ready, 1)
                dve.wait_ge(d_ready, 4 * gb + 2 * h + 1)
                dve.scalar_tensor_tensor(d, z, 1.0, d, ALU.add, ALU.mult).then_inc(d_ready, 1)
                dve.wait_ge(d_ready, 4 * gb + 2 * h + 2)
                dve.wait_ge(p_ready, 2 * gb + h + 1)
                part = half_of_x(at, h)
                dve.scalar_tensor_tensor(part, d, 0.5, part, ALU.mult, ALU.add).then_inc(out_ready, 1)

            def step(it, par, front, back, load=True):
                g = 2 * it + par
                gb = g - 1
                first = isinstance(it, int) and g == 0
                second = isinstance(it, int) and g == 1
                if first:
                    norm_stats(0, 0, 0)
                if back and not second:
                    finish(slot_two_before(it, par), hn[par], gb - 1, 1)
                if second:
                    for n in range(3):
                        gates_lo(n)
                elif back:
                    gathered_lo(gb)
                if front:
                    normalise(it, par, g)
                if first:
                    batch_norms()
                    scale_conv2()
                    small_weights()
                if back:
                    section_b(gb)
                if second:
                    gathered_lo(0)
                if front:
                    split_nodes(par, g, 0)
                    split_nodes(par, g, 1)
                if front:
                    bias_messages(g)
                if first:
                    copy_taps()
                if back:
                    outputs(gb, 0)
                if front:
                    distance_rows(g)
                if first:
                    halve_state()
                    sum_taps()
                    edge_weights(0, 0)
                    edge_weights(0, 1)
                    filters_lo(B)
                    edge_weights(0, 2)
                    leaves_lo(0, 0)
                    edge_weights(0, 3)
                    leaves_lo(0, 1)
                    leaves_lo(0, 2)
                    filters_lo(A)
                    norm_stats(0, 1, 1)
                    filters_lo(C)
                    return
                if back:
                    outputs(gb, 1)
                if front and load:
                    norm_stats(it + par, 1 - par, g + 1)
                if back:
                    relu_conv_lo(gb, 0)
                if front:
                    edge_weights(g, 0)
                for t in range(tiles):
                    if back:
                        bias_gates(gb, t)
                    if front and t in EDGE_AT:
                        edge_weights(g, EDGE_AT[t])
                    if back:
                        if t == 1:
                            relu_conv_lo(gb, 1)
                        if t in (2, 4, 6):
                            new_gates(gb, t // 2 - 1)
                    if front and t in (3, 5, 6):
                        leaves_lo(g, {3: 0, 5: 1, 6: 2}[t])
                    if back and t == 7:
                        new_gates(gb, t // 2)
                        finish(slot_before(it, par), hn[1 - par], gb, 0)
                if not front:
                    finish(slot_before(it, par), hn[1 - par], gb, 1)

            step(0, 0, True, False)
            step(0, 1, True, True)
            with dve.Fori(1, groups // 2 - 1) as it:
                for par in range(2):
                    step(it, par, True, True)
            step(groups // 2 - 1, 0, True, True)
            step(groups // 2 - 1, 1, True, True, load=False)
            step(groups // 2, 0, False, True)

        @block.tensor
        def _(pe):
            def products(out_ap, pairs, start, stop):
                terms = [t for lh, ll, rh, rl in pairs for t in ((lh, rh), (lh, rl), (ll, rh))]
                for n, (lhs, rhs) in enumerate(terms):
                    last = pe.matmul(out_ap, lhs, rhs, start=start and n == 0,
                                     stop=stop and n == len(terms) - 1)
                return last

            w_tap = raw2.rearrange("p (i k) -> p k i", k=TAPS)
            gate_order = (2, 0, 1)

            def turn(bank, sources, at=0):
                for n, src in enumerate(sources):
                    k = src.shape[0]
                    last = pe.transpose(bank[:, at + n * P:at + n * P + k], src, ident[0:k, 0:k])
                last.then_inc(w_turned, 1)

            def turn_small():
                pe.wait_ge(ident_ready, 1)
                pe.wait_ge(raw_scaled, 1)
                pe.wait_ge(small_in, 16 * 2)
                turn(gbk[0], [raw_c1, raw_msg, raw_se])

            def turn_taps(n):
                if n == 4:
                    pe.wait_ge(c1_ready, 2)
                    pe.wait_ge(ms_ready, 2)
                    turn(gbk[0], [w_tap[:, TAPS - 1, :]], 3 * P)
                else:
                    turn((gbk[1], cb[0], cb[1], cb[2])[n], [w_tap[:, 4 * n + k, :] for k in range(4)])

            def turn_gates():
                pe.wait_ge(taps_copied, 5)
                pe.wait_ge(raw_scaled, 3)
                turn(gate_raw_bank[GX], [raw_ih[:, k, 0:P] for k in gate_order])
                turn(gate_raw_bank[GN], [raw_ih[:, k, P:2 * P] for k in gate_order])
                turn(gate_raw_bank[GH], [raw_hh[:, k, :] for k in range(3)])

            freed = {T0: (hT_ready, 2, 1), T1: (hT_ready, 2, 2), M0: (msg_biased, 3, 1),
                     M1: (msg_biased, 3, 2), M2: (msg_biased, 3, 3), C0: (h1_ready, 4, 2),
                     C1: (h1_ready, 4, 4), SR: (rows_ready, 1, 1), N0: (nm_lo_ready, 2, 1),
                     N1: (nm_lo_ready, 2, 2)}
            for b in range(GB):
                freed[J[b]] = (edge_ready, GB, b + 1)
                freed[D[b]] = (exp_ready, GB, b + 1)

            def front_bank(use, g):
                before = use - 3
                s, per, n = freed[before % FRONT]
                wait(pe, s, per * (g - (before < 0)) + n)
                return fbk[use % 3]

            def conv(kind, section, leaves, release, released):
                wait(pe, release, released)
                for n, leaf in enumerate(leaves):
                    at, taps = leaf_at[section, leaf]
                    pairs = []
                    for k in range(taps):
                        hi, lo = (v[:, LEAF_SLOT[leaf], section * GB:(section + 1) * GB, k:k + quarter]
                                  for v in (leaf_hi, leaf_lo))
                        pairs.append((filt_hi[:, at + k, :], filt_lo[:, at + k, :], hi, lo))
                    width = GB * quarter
                    last = products(cb[kind % 3][:, n * width:(n + 1) * width], pairs, True, True)
                last.then_inc(conv_done, 1)

            def turn_nodes(par, g):
                for h in range(2):
                    bank = front_bank(T0 + h, g)
                    pe.wait_ge(hn_ready, 2 * g + h + 1)
                    for t in range(half_tiles):
                        last = pe.transpose(bank[:, t * P:(t + 1) * P], hn[par][:, h * half_tiles + t, :],
                                            ident[:])
                    last.then_inc(front_done, 1)

            def conv1(par, g):
                for h in range(2):
                    bank = front_bank(C0 + h, g)
                    pe.wait_ge(hT_split, 4 * g + 2 * h + 2)
                    cols = slice(h * 512, (h + 1) * 512)
                    products(bank[:], [(c1_hi[:], c1_lo[:], hT_hi[par][:, cols], hT_lo[par][:, cols])],
                             True, True).then_inc(front_done, 1)

            def messages(par, g):
                for n in range(3):
                    bank = front_bank(M0 + n, g)
                    pe.wait_ge(hT_ready, 2 * g + 2)
                    for t in range(3 * n, min(3 * n + 3, tiles)):
                        last = pe.matmul(bank[:, (t - 3 * n) * MS:(t - 3 * n + 1) * MS],
                                         hT[par][:, t * P:(t + 1) * P], w_ms[:], start=True, stop=True)
                    last.then_inc(front_done, 1)

            def turn_rows(g):
                bank = front_bank(SR, g)
                pe.wait_ge(stage_ready, g + 1)
                for n in range(4):
                    last = pe.transpose(bank[:, n * P:(n + 1) * P],
                                        stage[:, n // 2, n % 2].rearrange("p b r -> p (b r)"), ident[:])
                last.then_inc(front_done, 1)

            def graph_edges(g, b):
                bank = front_bank(D[b], g)
                pe.wait_ge(rows_ready, g + 1)
                mine = slice(SLOT * b, SLOT * b + KDIST)
                for mt in range(2):
                    last = pe.matmul(bank[:, mt * nodes:(mt + 1) * nodes],
                                     rows[mine, mt * P:(mt + 1) * P], rows[mine, 2 * P:4 * P],
                                     start=True, stop=True)
                last.then_inc(front_done, 1)
                bank = front_bank(J[b], g)
                pe.wait_ge(adj_in[b], 16 * (g + 1))
                for mt in range(2):
                    for nt in range(2):
                        last = pe.transpose(bank[:, mt * nodes + nt * P:mt * nodes + (nt + 1) * P],
                                            adj_sb[:, b, nt, mt * P:(mt + 1) * P], ident[:])
                last.then_inc(front_done, 1)

            def gather(g, h):
                bank = front_bank(N0 + h, g)
                pe.wait_ge(edge_ready, GB * g + 2 * h + 2)
                pe.wait_ge(msg_ready, 3 * g + 3)
                for b in (2 * h, 2 * h + 1):
                    for mt in range(2):
                        last = pe.matmul(bank[:, (b % 2) * nodes:(b % 2 + 1) * nodes],
                                         msg[:, 2 * b + mt, 0:P], edge[:, b, mt, :], start=mt == 0,
                                         stop=mt == 1)
                last.then_inc(front_done, 1)

            def gate_start(par, gb, t):
                if t in (2, 3, 4):
                    pe.wait_ge(*((y_ready, 2 * gb + 1), (p_copied, 3 * gb + 3), (y_ready, 2 * gb + 2))[t - 2])
                elif t >= 5:
                    pe.wait_ge(gate_biased, tiles * gb + t - 4)
                cols = slice(t * P, (t + 1) * P)
                bank = gate_bank[t]
                h_hi, h_lo = hT_hi[par][:, cols], hT_lo[par][:, cols]
                pe.matmul(bank[:], h_hi, gate_hi_wide, start=True, stop=False)
                pe.matmul(bank[:, P:4 * P], h_hi, gate_lo[:, GH], start=False, stop=False)
                pe.matmul(bank[:, P:4 * P], h_lo, gate_hi[GH], start=False, stop=False)
                if t == 0:
                    pe.wait_ge(nm_lo_ready, 2 * gb + 2)
                products(bank[:, 0:3 * P], [(nm_hi[:, cols], nm_lo[:, cols],
                                             gate_hi[GN], gate_lo[:, GN])], False, False)

            def gate_end(gb, t):
                cols = slice(t * P, (t + 1) * P)
                bank = gate_bank[t]
                if t in (0, half_tiles):
                    half = t // half_tiles
                    pe.wait_ge(xc_hi_ready, 2 * gb + half + 1)
                    pe.wait_ge(xc_lo_ready, 2 * gb + half + 1)
                products(bank[:, 0:3 * P], [(xc_hi[:, cols], xc_lo[:, cols],
                                             gate_hi[GX], gate_lo[:, GX])], False, True)\
                    .then_inc(gate_done, 1)

            def step(it, par, front, back):
                g = 2 * it + par
                gb = g - 1
                first = isinstance(it, int) and g == 0
                second = isinstance(it, int) and g == 1

                def need_filters(n):
                    if second:
                        pe.wait_ge(filt_hi_ready, n)
                        pe.wait_ge(filt_lo_ready, n)
                if back:
                    pe.wait_ge(leaf_hi_ready, LEAVES * gb + 1)
                    pe.wait_ge(leaf_lo_ready, LEAVES * gb + 1)
                    need_filters(1)
                    conv(CV_BB, B, (B,), gate_biased, tiles * gb)
                    pe.wait_ge(leaf_hi_ready, LEAVES * g)
                    pe.wait_ge(leaf_lo_ready, LEAVES * g)
                    need_filters(3)
                    conv(CV_B, B, (A, C), p_copied, 3 * gb)
                    if second:
                        gather(0, 0)
                        gather(0, 1)
                        pe.wait_ge(gate_lo_ready, 3)
                    need_filters(4)
                    conv(CV_AB, A, (B,), gate_biased, tiles * gb)
                    need_filters(6)
                    conv(CV_A, A, (A, C), p_copied, 3 * gb + 1)
                if front:
                    turn_nodes(par, g)
                if first:
                    turn_small()
                    pe.wait_ge(raw_scaled, 2)
                    turn_taps(0)
                    pe.wait_ge(ms_ready, 2)
                if back:
                    need_filters(7)
                    conv(CV_CB, C, (B,), mb_ready, gb + 1)
                if front:
                    messages(par, g)
                if back:
                    need_filters(9)
                    conv(CV_C, C, (A, C), p_copied, 3 * gb + 2)
                if first:
                    for n in (1, 2, 3):
                        turn_taps(n)
                    pe.wait_ge(c1_ready, 2)
                if front:
                    conv1(par, g)
                if first:
                    turn_taps(4)
                    pe.wait_ge(zero_ready, ZEROS)
                if first:
                    turn_gates()
                if front:
                    turn_rows(g)
                if back:
                    gate_start(1 - par, gb, 0)
                    gate_start(1 - par, gb, 1)
                if front:
                    graph_edges(g, 0)
                if back:
                    gate_start(1 - par, gb, 2)
                    gate_end(gb, 0)
                if front:
                    graph_edges(g, 1)
                if back:
                    gate_end(gb, 1)
                for t in range(2, tiles):
                    if back:
                        if t > 2:
                            gate_start(1 - par, gb, t)
                        gate_end(gb, t)
                    if front and t in (2, 4):
                        graph_edges(g, 2 if t == 2 else 3)
                if front and not first:
                    gather(g, 0)
                    gather(g, 1)

            steps(pe, step)


_INS = ["x", "adj"] + ["L0_gnn_" + n for n in (
    "w_se", "b_se", "conv1_w", "bn1_g", "bn1_b", "bn1_m", "bn1_v", "conv2_w", "bn2_g", "bn2_b", "bn2_m",
    "bn2_v", "w_msg", "b_msg", "w_ih", "b_ih", "w_hh", "b_hh")]


def kernel(**inputs):
    import numpy as np
    import concourse.bacc as bacc
    from concourse.bass_utils import run_bass_kernel_spmd

    nc = bacc.Bacc("TRN2", target_bir_lowering=False, num_devices=1)
    arrays, args = {}, []
    for name in _INS:
        a = np.ascontiguousarray(inputs[name])
        arrays[f"in_{name}"] = a
        args.append(nc.dram_tensor(f"in_{name}", a.shape, F32, kind="ExternalInput").ap())
    shape = arrays["in_x"].shape
    out = nc.dram_tensor("out_0", shape, F32, kind="ExternalOutput").ap()
    build(nc, *args, out)
    r = run_bass_kernel_spmd(nc, [arrays], core_ids=[0])
    return r.results[0]["out_0"]
```
